# Optimizing a Trainium2 kernel written in Bass

```python
import numpy as np
import jax
import jax.numpy as jnp

def _softmax(x, axis=-1):
    return jax.nn.softmax(x, axis=axis)

def _gelu(x):
    return jax.nn.gelu(x, approximate=True)

def _silu(x):
    return jax.nn.silu(x)

def _sigmoid(x):
    return jax.nn.sigmoid(x)

def _layernorm(x, axis=-1, eps=1e-05):
    m = jnp.mean(x, axis=axis, keepdims=True)
    v = jnp.var(x, axis=axis, keepdims=True)
    return (x - m) / jnp.sqrt(v + eps)

def _scatter_add(tgt, idx, src, axis=0):
    return tgt.at[idx].add(src)

def _segment_sum(src, seg, n):
    return jax.ops.segment_sum(src, seg, n)
kernel_name = 'mk_flamingo_gated_d1_seqx_r4_2bcc33'

def setup_inputs(seed: int=0):
    np.random.seed(seed)
    _w = jnp.asarray

    def _rec_inputs():
        import jax
        import jax.numpy as jnp
        _rk = jax.random.key(seed)
        x = -0.0002928 + 1 * jax.random.normal(jax.random.fold_in(_rk, 1), (8, 256, 512), jnp.float32)
        _lenS = 256 - jax.random.randint(jax.random.fold_in(_rk, 7), (8,), 0, max(1, 256 // 4) + 1, jnp.int32)
        _lenS2 = 256 - jax.random.randint(jax.random.fold_in(_rk, 8), (8,), 0, max(1, 256 // 4) + 1, jnp.int32)
        _ctx_2048P = jax.random.normal(jax.random.fold_in(_rk, 11), (8, 16, 512), jnp.float32)
        _ctx_2048c = jax.random.dirichlet(jax.random.fold_in(_rk, 511), 0.3 * jnp.ones((16,), jnp.float32), (8, 256))
        _ctx_2048t = jnp.einsum('bsk,bkd->bsd', _ctx_2048c, _ctx_2048P)
        _ctx_2048t = _ctx_2048t * jax.lax.rsqrt(jnp.mean(jnp.square(_ctx_2048t)) + 1e-12) * 0.953939
        ctx_2048 = -1.39393e-06 + 0.999914 * (_ctx_2048t + 0.3 * jax.random.normal(jax.random.fold_in(_rk, 611), (8, 256, 512), jnp.float32))
        _validS = jnp.arange(256)[None, :] < _lenS[:, None]
        _validS2 = jnp.arange(256)[None, :] < _lenS2[:, None]
        _causal = jnp.tril(jnp.ones((256, 256), dtype=bool))
        mask_Bx1x2048_fk1 = jnp.where(jnp.ones((8, 1, 512), dtype=bool), 1.0, 0.0).astype(jnp.float32)
        _g = jax.random.normal(jax.random.fold_in(_rk, 9001), (2, 1), jnp.float32)
        _g = jnp.sign(_g) * jnp.maximum(jnp.abs(_g), 1.0) + (_g == 0) * 1.0
        g_xattn = _g[0]
        g_ffn = _g[1]
        return (x, ctx_2048, mask_Bx1x2048_fk1, g_xattn, g_ffn)
    x, ctx_2048, mask_Bx1x2048_fk1, g_xattn, g_ffn = _rec_inputs()

    def _L0_xattn_setup():
        import math
        import jax, jax.numpy as jnp
        import numpy as np
        SIZE = 256
        HEADS = 16
        HEAD_DIM = SIZE // HEADS
        B, T, S = (2, 512, 512)
        NEG = 1000000.0
        key = jax.random.key(seed)
        ks = jax.random.split(key, 10)
        target = jax.random.normal(ks[0], (B, SIZE, T), dtype=jnp.float32)
        source = jax.random.normal(ks[1], (B, SIZE, S), dtype=jnp.float32)
        target_mask = (jax.random.uniform(ks[2], (B, 1, T)) > 0.1).astype(jnp.float32)
        source_mask = (jax.random.uniform(ks[3], (B, 1, S)) > 0.1).astype(jnp.float32)
        scale = 1.0 / math.sqrt(SIZE)
        Wq = jax.random.normal(ks[4], (SIZE, SIZE), dtype=jnp.float32) * scale
        Wk = jax.random.normal(ks[5], (SIZE, SIZE), dtype=jnp.float32) * scale
        Wv = jax.random.normal(ks[6], (SIZE, SIZE), dtype=jnp.float32) * scale
        bq = jax.random.normal(ks[7], (SIZE,), dtype=jnp.float32) * 0.01
        bk = jax.random.normal(ks[8], (SIZE,), dtype=jnp.float32) * 0.01
        bv = jax.random.normal(ks[9], (SIZE,), dtype=jnp.float32) * 0.01
        return {'target': target, 'source': source, 'target_mask': target_mask, 'source_mask': source_mask, 'Wq': Wq, 'bq': bq, 'Wk': Wk, 'bk': bk, 'Wv': Wv, 'bv': bv}
    _L0_xattn_all = _L0_xattn_setup()
    _L0_xattn_in = {k: v for k, v in _L0_xattn_all.items() if k in ('Wq', 'bq', 'Wk', 'bk', 'Wv', 'bv')}
    del _L0_xattn_all

    def _L0_ffn_setup():
        import jax, jax.numpy as jnp
        import numpy as np
        TOPK = 2
        key = jax.random.key(seed)
        ks = jax.random.split(key, 6)
        B, T, H, S, r, ad = (2, 1024, 512, 32, 16, 32)
        h = jax.random.normal(ks[0], (B, T, H), dtype=jnp.float32)
        Wr = jax.random.normal(ks[1], (S, H), dtype=jnp.float32) * 0.02
        U = jax.random.normal(ks[2], (S, H, r), dtype=jnp.float32) * 0.02
        V = jax.random.normal(ks[3], (S, r, H), dtype=jnp.float32) * 0.02
        attr = jax.random.normal(ks[4], (S, ad), dtype=jnp.float32) * 0.02
        Wa = jax.random.normal(ks[5], (1, ad), dtype=jnp.float32) * 0.02
        return {'h': h, 'Wr': Wr, 'U': U, 'V': V, 'attr': attr, 'Wa': Wa}
    _L0_ffn_all = _L0_ffn_setup()
    _L0_ffn_in = {k: v for k, v in _L0_ffn_all.items() if k in ('Wr', 'U', 'V', 'attr', 'Wa')}
    del _L0_ffn_all
    return {'x': x, 'ctx_2048': ctx_2048, 'mask_Bx1x2048_fk1': mask_Bx1x2048_fk1, 'g_xattn': g_xattn, 'g_ffn': g_ffn, 'L0_xattn_Wq': _L0_xattn_in['Wq'], 'L0_xattn_bq': _L0_xattn_in['bq'], 'L0_xattn_Wk': _L0_xattn_in['Wk'], 'L0_xattn_bk': _L0_xattn_in['bk'], 'L0_xattn_Wv': _L0_xattn_in['Wv'], 'L0_xattn_bv': _L0_xattn_in['bv'], 'L0_ffn_Wr': _L0_ffn_in['Wr'], 'L0_ffn_U': _L0_ffn_in['U'], 'L0_ffn_V': _L0_ffn_in['V'], 'L0_ffn_attr': _L0_ffn_in['attr'], 'L0_ffn_Wa': _L0_ffn_in['Wa']}

def reference(x, ctx_2048, mask_Bx1x2048_fk1, g_xattn, g_ffn, L0_xattn_Wq, L0_xattn_bq, L0_xattn_Wk, L0_xattn_bk, L0_xattn_Wv, L0_xattn_bv, L0_ffn_Wr, L0_ffn_U, L0_ffn_V, L0_ffn_attr, L0_ffn_Wa):
    import jax
    import jax.numpy as jnp

    def _L0_xattn_ref(target, source, target_mask, source_mask, Wq, bq, Wk, bk, Wv, bv):
        import math
        import jax, jax.numpy as jnp
        import numpy as np
        SIZE = 256
        HEADS = 16
        HEAD_DIM = SIZE // HEADS
        B, T, S = (2, 512, 512)
        NEG = 1000000.0
        b, _, t = target.shape
        s = source.shape[-1]
        q = jnp.einsum('oc,bct->bot', Wq, target) + bq[None, :, None]
        k = jnp.einsum('oc,bcs->bos', Wk, source) + bk[None, :, None]
        v = jnp.einsum('oc,bcs->bos', Wv, source) + bv[None, :, None]
        q = q.reshape(b, HEADS, HEAD_DIM, t)
        k = k.reshape(b, HEADS, HEAD_DIM, s)
        v = v.reshape(b, HEADS, HEAD_DIM, s)
        dot = jnp.einsum('bhdt,bhds->bhts', q, k) / math.sqrt(HEAD_DIM)
        mask = target_mask[:, :, :, None] * source_mask[:, :, None, :]
        dot = mask * dot - (1.0 - mask) * NEG
        amap = jax.nn.softmax(dot, axis=-1) * mask
        out = jnp.einsum('bhts,bhds->bhdt', amap, v)
        return out.reshape(b, HEADS * HEAD_DIM, t)

    def _L0_ffn_ref(h, Wr, U, V, attr, Wa):
        import jax, jax.numpy as jnp
        import numpy as np
        TOPK = 2
        S = Wr.shape[0]
        sc = jnp.einsum('bth,sh->bts', h, Wr)
        _, idx = jax.lax.top_k(sc, TOPK)
        m = jax.nn.one_hot(idx, S, dtype=sc.dtype).sum(axis=-2)
        g = jax.nn.softmax(sc, axis=-1) * m
        g = g / (g.sum(axis=-1, keepdims=True) + 1e-08)
        hU = jnp.einsum('bth,shr->btsr', h, U)
        out = jnp.einsum('bts,btsr,srh->bth', g, hU, V)
        aw = jax.nn.sigmoid(attr @ Wa[0])
        gate = (g @ aw)[..., None]
        return out * (0.9 + 0.2 * gate)
    x = x + jnp.tanh(g_xattn[0]) * _L0_xattn_ref(_layernorm(x, axis=-1), ctx_2048, mask_Bx1x2048_fk1, mask_Bx1x2048_fk1, L0_xattn_Wq, L0_xattn_bq, L0_xattn_Wk, L0_xattn_bk, L0_xattn_Wv, L0_xattn_bv)
    x = x + jnp.tanh(g_ffn[0]) * _L0_ffn_ref(_layernorm(x, axis=-1), L0_ffn_Wr, L0_ffn_U, L0_ffn_V, L0_ffn_attr, L0_ffn_Wa)
    return x

_drawn_inputs = setup_inputs


def setup_inputs(seed=0):
    import zlib

    import numpy as np

    out = dict(_drawn_inputs(seed))
    spreads = {}
    factors = {'L0_xattn_bq': 22.044,
     'L0_xattn_bk': 64.0,
     'L0_xattn_bv': 7.416,
     'L0_ffn_attr': 64.0,
     'L0_ffn_Wa': 64.0}
    for name, (base, spread) in spreads.items():
        noise = np.random.default_rng([zlib.crc32(name.encode()), seed]).standard_normal(out[name].shape)
        drawn = base * np.exp(spread * noise) if base else spread * noise
        out[name] = jnp.asarray(drawn.astype(out[name].dtype))
    for name, factor in factors.items():
        out[name] = (out[name] * factor).astype(out[name].dtype)
    return out
```

```python
import concourse.bass as bass
from concourse import mybir
from contextlib import ExitStack

F32 = mybir.dt.float32
F32R = mybir.dt.float32r
ALU = mybir.AluOpType
ACT = mybir.ActivationFunctionType
AX_X = mybir.AxisListType.X

B, C, T = 8, 256, 512
D = 16
HG = 4
NG = 4
NT = T // 128
NC = C // 128
UNITS = HG * NT
E_, R = 32, 16
WU_COLS = E_ + E_ * R
FHALF = WU_COLS // 2
S0 = (FHALF - E_) // R
NEG = -1000000.0
EPS = 1e-5
CONSTS = 14
ZEROED = 6
LOAD_DMAS = 10
SENT = -3.0e38
PICK = 3.0e38


def build(nc, x, ctx_, mask, mask_cols, g_x, g_f, wqT, wkT, wvT, bq, bk, bv, wu, v2, attr, wa, out):
    with ExitStack() as st_:
        def sb(name, shape, dt=F32):
            return st_.enter_context(nc.sbuf_tensor(name, shape, dt))

        def sem(name):
            return st_.enter_context(nc.semaphore(name))

        def scratch(name, shape):
            return nc.dram_tensor(name, shape, F32, kind="Internal").ap()

        q_parts = scratch("q_parts", (B * 2 * C, T))
        k_parts = scratch("k_parts", (B * 2 * C, T))
        q_mask_rows = scratch("q_mask_rows", (B * 4, T))
        k_mask_rows = scratch("k_mask_rows", (B * 4, T))
        max_rows = scratch("max_rows", (B * NG * 32, 128))

        ident = sb("ident", [128, 128])
        wq_sb = sb("wq_sb", [128, NC, C])
        wk_sb = sb("wk_sb", [128, NC, C])
        wv_sb = sb("wv_sb", [128, NC, C])
        bq_sb = sb("bq_sb", [128, NC])
        bk_sb = sb("bk_sb", [128, NC])
        bv_sb = sb("bv_sb", [128, C])
        wu_sb = sb("wu_sb", [128, NT, WU_COLS])
        v2_sb = sb("v2_sb", [128, NT, T])
        wa_sb = sb("wa_sb", [128, E_])
        gates = sb("gates", [128, 2])
        tanh_g = sb("tanh_g", [128, 2])
        aw = sb("aw", [128, E_])
        aw_lin = sb("aw_lin", [128, E_])
        aw_th = sb("aw_th", [128, E_])
        mcols = sb("mcols", [128, B * NT])
        tm_gate = sb("tm_gate", [128, B * NT])
        minus_half = sb("minus_half", [128, NC])
        carrier = sb("carrier", [1, 16])
        eps_sb = sb("eps_sb", [128, NC])
        m8 = sb("m8", [B, T])
        m8_full = sb("m8_full", [B, 2, T])
        m8_hi = sb("m8_hi", [B, 2, T], F32R)
        m8_lo = sb("m8_lo", [B, 2, T], F32R)

        x_sb = sb("x_sb", [128, NC, T])
        xn = sb("xn", [128, NC, T])
        ctx_sb = sb("ctx_sb", [128, NC, T])
        mask_bc = sb("mask_bc", [128, T])
        qf = sb("qf", [128, T])
        kf = sb("kf", [128, T])
        q_hi = sb("q_hi", [128, T], F32R)
        q_lo = sb("q_lo", [128, T], F32R)
        k_hi = sb("k_hi", [128, T], F32R)
        k_lo = sb("k_lo", [128, T], F32R)
        qa = sb("qa", [128, NG, HG, T], F32R)
        ka = sb("ka", [128, NG, HG, T], F32R)
        probs = sb("probs", [128, 2, HG, T])
        v_biased = sb("v_biased", [128, NT, C])
        v_masked = sb("v_masked", [128, NT, C])
        v_ext = sb("v_ext", [128, NG, NT, HG, 32])
        neg_max = sb("neg_max", [128, 2, UNITS])
        neg_max_parts = sb("neg_max_parts", [128, 2 * UNITS], F32R)
        neg_max_T = sb("neg_max_T", [2 * UNITS, 128], F32R)
        pv_sb = sb("pv_sb", [128, T])
        rsum = sb("rsum", [128, NT, HG])
        rscale = sb("rscale", [128, NT, HG])
        attn_T = sb("attn_T", [128, NT, 128])
        x_res = sb("x_res", [128, T])
        xp = sb("xp", [128, T])
        h_sb = sb("h_sb", [128, T])
        hT = sb("hT", [128, NT, 128])
        z = sb("z", [128, T])
        zT = sb("zT", [128, NT, 128])
        y = sb("y", [128, T])
        stats = sb("stats", [128, NC, 6])
        mv = sb("mv", [128, NC, 2])
        rstd = sb("rstd", [128, NC])
        var_eps = sb("var_eps", [128, NC])
        mean_rstd = sb("mean_rstd", [128, NC])
        stats2 = sb("stats2", [128, 6])
        mv2 = sb("mv2", [128, 2])
        rstd2 = sb("rstd2", [128, 1])
        var_eps2 = sb("var_eps2", [128, 1])
        mean_rstd2 = sb("mean_rstd2", [128, 1])
        scores = sb("scores", [128, E_ + 8])
        top8 = sb("top8", [128, 8])
        top2 = sb("top2", [128, 8])
        neg_top = sb("neg_top", [128, 1])
        picked = sb("picked", [128, E_ + 8])
        escore = sb("escore", [128, E_])
        esum = sb("esum", [128, 1])
        epick = sb("epick", [128, E_])
        epick_sum = sb("epick_sum", [128, 1])
        eaw = sb("eaw", [128, E_])
        eaw_sum = sb("eaw_sum", [128, 1])
        den = sb("den", [128, 1])
        rden = sb("rden", [128, 1])
        gate_part = sb("gate_part", [128, 1])
        wscale = sb("wscale", [128, 1])
        gs = sb("gs", [128, E_])

        def bank(name):
            return st_.enter_context(nc.psum_tensor(name, [128, 512], F32))

        max_bank = [bank(f"max_bank{i}") for i in range(2)]
        exp_bank = [bank(f"exp_bank{i}") for i in range(2)]
        pv_bank = [bank(f"pv_bank{i}") for i in range(2)]
        bankA, bankB = bank("bankA"), bank("bankB")

        const_loaded = sem("const_loaded")
        zeroed = sem("zeroed")
        ident_ready = sem("ident_ready")
        setup_act = sem("setup_act")
        setup_vec = sem("setup_vec")
        mask_rows_stored = sem("mask_rows_stored")
        x_loaded = sem("x_loaded")
        ctx_loaded = sem("ctx_loaded")
        mask_loaded = sem("mask_loaded")
        parts_stored = sem("parts_stored")
        slot_loaded = [sem(f"slot_loaded{g}") for g in range(NG)]
        max_stored = sem("max_stored")
        max_loaded = [sem(f"max_loaded{g}") for g in range(NG)]
        xres_loaded = sem("xres_loaded")
        y_stored = sem("y_stored")
        q_proj, k_proj, v_proj = sem("q_proj"), sem("k_proj"), sem("v_proj")
        max_logits, exp_logits = sem("max_logits"), sem("exp_logits")
        pv_step = sem("pv_step")
        max_T, pv_T, attn_back, h_T, ffn_in, z_T, ffn_out = (
            sem(n) for n in ("max_T", "pv_T", "attn_back", "h_T", "ffn_in", "z_T", "ffn_out"))
        exp_done = sem("exp_done")
        max_T_copied, pv_copied, hT_copied, zT_copied = (
            sem(n) for n in ("max_T_copied", "pv_copied", "hT_copied", "zT_copied"))
        escore_done = sem("escore_done")
        max_done = sem("max_done")
        max_hi, max_parts = sem("max_hi"), sem("max_parts")
        stats_done, mv_done = sem("stats_done"), sem("mv_done")
        q_biased, k_biased, v_biased_done = sem("q_biased"), sem("k_biased"), sem("v_biased_done")
        norm_step, attn_normed = sem("norm_step"), sem("attn_normed")
        xp_done, stats2_done, mv2_done = sem("xp_done"), sem("stats2_done"), sem("mv2_done")
        neg_top_done, router_step, z_done, y_done = (
            sem("neg_top_done"), sem("router_step"), sem("z_done"), sem("y_done"))
        ln_step, xn_done = sem("ln_step"), sem("xn_done")
        parts_split = sem("parts_split")
        v_masked_done, v_ready = sem("v_masked_done"), sem("v_ready")
        ln2_step, h_done = sem("ln2_step"), sem("h_done")

        def wait(eng, s, value):
            if isinstance(value, int) and value <= 0:
                return
            eng.wait_ge(s, value)

        def wait_apart(eng, place, *waits):
            for s, value in waits:
                wait(eng, s, value)
            element = carrier[0:1, place:place + 1]
            if eng is nc.gpsimd:
                eng.tensor_tensor(element, minus_half[0:1, 0:1], minus_half[0:1, 0:1], ALU.mult)
            else:
                eng.memset(element, 0.0)

        def before(b, g):
            return (b, g - 1) if g else (b - 1, NG - 1)

        def ahead(b, g):
            return (b, g + 2) if g < 2 else (b + 1, g - 2)

        def batches(eng, body, peeled=1):
            for b in range(peeled):
                body(b, b == 0, False)
            with eng.Fori(peeled, B - 1) as b:
                body(b, False, False)
            body(B - 1, False, True)

        block = st_.enter_context(nc.Block())

        @block.sync
        def _(sp):
            CONST = [
                (wq_sb[:], wqT.rearrange("(c p) o -> p c o", p=128)),
                (bq_sb[:], bq), (mcols[:], mask_cols),
                (m8[:], mask.rearrange("b o t -> (b o) t")),
            ]
            LATER = [
                (wk_sb[:], wkT.rearrange("(c p) o -> p c o", p=128)),
                (bk_sb[:], bk),
                (wv_sb[:], wvT.rearrange("(c p) o -> p c o", p=128)),
                (bv_sb[:], bv.partition_broadcast(128)),
                (gates[:, 0:1], g_x.partition_broadcast(128)),
                (gates[:, 1:2], g_f.partition_broadcast(128)),
                (probs[:, 0, 0:2, :].rearrange("p a t -> p (a t)"),
                 attr.rearrange("s a -> (s a)").partition_broadcast(128)),
                (wa_sb[:], wa.rearrange("o a -> (o a)").partition_broadcast(128)),
                (wu_sb[:], wu.rearrange("(k p) n -> p k n", p=128)),
                (v2_sb[:], v2.rearrange("(k p) n -> p k n", p=128)),
            ]

            def load_x(b):
                wait(sp, xn_done, b * 2)
                rows = x[bass.ds(b * C, C), :]
                sp.dma_start(x_sb[:], rows.rearrange("(c p) t -> p c t", p=128)).then_inc(x_loaded, 16)

            def load_ctx(b):
                wait(sp, k_proj, b * 2)
                wait(sp, v_proj, b * 2)
                rows = ctx_[bass.ds(b * C, C), :]
                sp.dma_start(ctx_sb[:], rows.rearrange("(c p) t -> p c t", p=128)).then_inc(ctx_loaded, 16)
                wait(sp, q_biased, b * 2)
                wait(sp, k_biased, b * 2)
                row = mask[bass.ds(b, 1)].rearrange("b o t -> (b o t)").partition_broadcast(128)
                sp.dma_start(mask_bc[:], row).then_inc(mask_loaded, 16)

            def load_xres(h):
                wait(sp, xp_done, h)
                sp.dma_start(x_res[:], x[bass.ds(h * 128, 128), :]).then_inc(xres_loaded, 16)

            def store_parts(b, ct):
                wait(sp, parts_split, b * 8 + (ct * 4 + 4))
                for dst, tiles in ((q_parts, (q_hi, q_lo)), (k_parts, (k_hi, k_lo))):
                    for hl, tile in enumerate(tiles):
                        rows = dst[bass.ds(b * (2 * C) + (hl * C + ct * 128), 128), :]
                        sp.dma_start(rows, tile[:].bitcast(F32)).then_inc(parts_stored, 16)

            def load_slot(b, g):
                wait(sp, parts_stored, b * 128 + (g // 2 + 1) * 64)
                wait(sp, exp_logits, (b * NG + (g + 1 - NG)) * UNITS)
                for side, src, order in ((qa, q_parts, (0, 0, 1, 1)), (ka, k_parts, (0, 1, 0, 1))):
                    for r, hl in enumerate(order):
                        rows = src[bass.ds(b * (2 * C) + (hl * C + g * HG * D), HG * D), :]
                        sp.dma_start(side[r * D:(r + 1) * D, g].bitcast(F32),
                                     rows.rearrange("(j d) t -> d j t", j=HG)).then_inc(slot_loaded[g], 16)
                for side, src in ((qa, q_mask_rows), (ka, k_mask_rows)):
                    rows = src[bass.ds(b * 4, 4), :].unsqueeze(1).to_broadcast([4, HG, T])
                    sp.dma_start(side[64:68, g].bitcast(F32), rows).then_inc(slot_loaded[g], 16)

            def max_to_rows(b, g):
                G = b * NG + g
                wait(sp, max_T_copied, G + 1)
                rows = max_rows[bass.ds(G * 32, 32), :]
                sp.dma_start(rows, neg_max_T[:].bitcast(F32)).then_inc(max_stored, 16)
                wait(sp, max_stored, (G + 1) * 16)
                sp.dma_start(qa[96:98, g].bitcast(F32),
                             rows.rearrange("(h j tt) t -> h j (tt t)", h=2, j=HG)).then_inc(max_loaded[g], 16)

            def store_y(h):
                wait(sp, y_done, h + 1)
                sp.dma_start(out[bass.ds(h * 128, 128), :], y[:]).then_inc(y_stored, 16)

            load_x(0)
            for dst, src in CONST:
                sp.dma_start(dst, src).then_inc(const_loaded, 16)
            load_ctx(0)
            for dst, src in LATER:
                sp.dma_start(dst, src).then_inc(const_loaded, 16)
            wait(sp, setup_vec, 5)
            for r in range(4):
                sp.dma_start(q_mask_rows.rearrange("(b r) t -> b r t", r=4)[:, r, :],
                             (m8_hi, m8_lo)[r % 2][:, 0, :].bitcast(F32)).then_inc(mask_rows_stored, 16)
                sp.dma_start(k_mask_rows.rearrange("(b r) t -> b r t", r=4)[:, r, :],
                             (m8_hi, m8_lo)[r // 2][:, 1, :].bitcast(F32)).then_inc(mask_rows_stored, 16)
            wait(sp, mask_rows_stored, 128)
            wait(sp, zeroed, ZEROED)
            store_parts(0, 0)
            load_slot(0, 0)
            load_slot(0, 1)
            load_x(1)
            store_parts(0, 1)
            load_slot(0, 2)
            load_slot(0, 3)
            load_ctx(1)
            max_to_rows(0, 0)

            def body(b, first, last, inputs_left):
                if not first:
                    load_slot(b, 3)
                    load_xres(b * 2 - 1)
                max_to_rows(b, 1)
                if not first:
                    store_y(b * 2 - 2)
                max_to_rows(b, 2)
                if not last:
                    store_parts(b + 1, 0)
                    load_slot(b + 1, 0)
                if inputs_left:
                    load_x(b + 2)
                load_xres(b * 2)
                max_to_rows(b, 3)
                if not last:
                    load_slot(b + 1, 1)
                if not first:
                    store_y(b * 2 - 1)
                if not last:
                    max_to_rows(b + 1, 0)
                    store_parts(b + 1, 1)
                    load_slot(b + 1, 2)
                if inputs_left:
                    load_ctx(b + 2)

            body(0, True, False, True)
            with sp.Fori(1, B - 2) as b:
                body(b, False, False, True)
            body(B - 2, False, False, False)
            body(B - 1, False, True, False)
            load_xres(B * 2 - 1)
            store_y(B * 2 - 2)
            store_y(B * 2 - 1)
            sp.wait_ge(y_stored, B * NC * 16)

        @block.gpsimd
        def _(pool):
            pool.memset(ident[:], 0.0).then_inc(ident_ready, 1)
            pool.wait_ge(ident_ready, 1)
            pool.affine_select(out=ident[:], in_=ident[:], compare_op=ALU.not_equal, fill=1.0, base=0,
                               pattern=[[-1, 128]], channel_multiplier=1).then_inc(ident_ready, 1)
            pool.memset(minus_half[:], -0.5).then_inc(ident_ready, 1)
            pool.memset(eps_sb[:], EPS).then_inc(ident_ready, 1)
            pool.wait_ge(ident_ready, 4)

            def normalise_x(b):
                wait(pool, mv_done, b * 2 + 2)
                wait(pool, xn_done, b * 2)
                pool.tensor_tensor(var_eps[:], mv[:, :, 1], eps_sb[:], ALU.add).then_inc(ln_step, 1)
                pool.wait_ge(ln_step, b * 3 + 1)
                pool.tensor_tensor(rstd[:], var_eps[:], minus_half[:], ALU.pow).then_inc(ln_step, 1)
                pool.wait_ge(ln_step, b * 3 + 2)
                pool.tensor_tensor(mean_rstd[:], mv[:, :, 0], rstd[:], ALU.mult).then_inc(ln_step, 1)
                wait_apart(pool, 0, (ln_step, b * 3 + 3), (q_proj, b * 2))
                for ct in range(NC):
                    pool.tensor_scalar(xn[:, ct], x_sb[:, ct], rstd[:, ct:ct + 1], mean_rstd[:, ct:ct + 1],
                                       ALU.mult, ALU.subtract).then_inc(xn_done, 1)

            def split(b, ct):
                n = b * 8 + ct * 4
                for i, (full, hi, lo, ready) in enumerate(((qf, q_hi, q_lo, q_biased), (kf, k_hi, k_lo, k_biased))):
                    wait_apart(pool, 2 + i, (ready, b * 2 + (ct + 1)), (parts_stored, (b * 2 + ct) * 64))
                    pool.tensor_copy(hi[:], full[:]).then_inc(parts_split, 1)
                    pool.wait_ge(parts_split, n + (2 * i + 1))
                    pool.tensor_tensor(lo[:], full[:], hi[:].bitcast(F32), ALU.subtract).then_inc(parts_split, 1)

            def mask_v(b):
                pool.wait_ge(v_biased_done, b * 2 + 2)
                wait(pool, v_ready, b * NG)
                sm = mcols[:, bass.ds(b * NT, NT)].unsqueeze(2).to_broadcast([128, NT, C])
                pool.tensor_tensor(v_masked[:], v_biased[:], sm, ALU.mult).then_inc(v_masked_done, 1)

            def place_v(b, g):
                wait_apart(pool, 4 + g, (v_masked_done, b + 1), (pv_step, (b * NG + (g + 1 - NG)) * NT))
                src = v_masked[:, :, g * HG * D:(g + 1) * HG * D].rearrange("p s (j d) -> p s j d", j=HG)
                pool.tensor_copy(v_ext[:, g, :, :, 0:D], src).then_inc(v_ready, 1)

            def normalise_xp(h):
                wait(pool, mv2_done, h + 1)
                wait(pool, h_done, h)
                pool.tensor_tensor(var_eps2[:], mv2[:, 1:2], eps_sb[:, 0:1], ALU.add).then_inc(ln2_step, 1)
                pool.wait_ge(ln2_step, h * 3 + 1)
                pool.tensor_tensor(rstd2[:], var_eps2[:], minus_half[:, 0:1], ALU.pow).then_inc(ln2_step, 1)
                pool.wait_ge(ln2_step, h * 3 + 2)
                pool.tensor_tensor(mean_rstd2[:], mv2[:, 0:1], rstd2[:], ALU.mult).then_inc(ln2_step, 1)
                wait_apart(pool, 1, (ln2_step, h * 3 + 3), (h_T, h))
                pool.tensor_scalar(h_sb[:], xp[:], rstd2[:], mean_rstd2[:], ALU.mult, ALU.subtract).then_inc(h_done, 1)

            normalise_x(0)
            pool.memset(v_ext[:, :, :, :, D + 1:32], 0.0).then_inc(zeroed, 1)
            pool.memset(v_ext[:, :, :, :, D:D + 1], 1.0).then_inc(zeroed, 1)
            split(0, 0)
            split(0, 1)
            mask_v(0)
            for g in range(NG - 1):
                place_v(0, g)

            def body(b, first, last):
                if not last:
                    normalise_x(b + 1)
                place_v(b, NG - 1)
                if not last:
                    split(b + 1, 0)
                if not first:
                    normalise_xp(b * 2 - 1)
                if not last:
                    mask_v(b + 1)
                    place_v(b + 1, 0)
                    place_v(b + 1, 1)
                    split(b + 1, 1)
                normalise_xp(b * 2)
                if not last:
                    place_v(b + 1, 2)

            batches(pool, body)
            normalise_xp(B * 2 - 1)

        @block.scalar
        def _(act):
            def exp_step(b, g, s):
                G = b * NG + g
                S = G * NT + s
                wait(act, pv_step, S - 1)
                for j in range(HG):
                    act.wait_ge(exp_logits, S * HG + (j + 1))
                    act.activation(probs[:, s % 2, j], exp_bank[j % 2][:], ACT.Exp).then_inc(exp_done, 1)

            def copy_max_T(b, g):
                G = b * NG + g
                act.wait_ge(max_T, G + 1)
                wait(act, max_stored, G * 16)
                src = (bankA, bankB)[g % 2]
                act.activation(neg_max_T[:], src[0:2 * UNITS, 0:128], ACT.Copy).then_inc(max_T_copied, 1)

            def copy_pv(b, g):
                G = b * NG + g
                act.wait_ge(pv_step, G * NT + NT)
                wait(act, pv_T, G)
                act.activation(pv_sb[:], pv_bank[g % 2][:], ACT.Copy).then_inc(pv_copied, 1)

            def copy_hT(h):
                act.wait_ge(h_T, h + 1)
                wait(act, ffn_in, h)
                act.activation(hT[:].rearrange("p k c -> p (k c)"), bankA[:], ACT.Copy).then_inc(hT_copied, 1)

            def exp_scores(h):
                act.wait_ge(neg_top_done, h + 1)
                act.activation(escore[:], scores[:, 0:E_], ACT.Exp, bias=neg_top[:], accum_out=esum[:])\
                   .then_inc(escore_done, 1)

            def copy_zT(h):
                act.wait_ge(z_T, h + 1)
                wait(act, ffn_out, h)
                act.activation(zT[:].rearrange("p k c -> p (k c)"), bankA[:], ACT.Copy).then_inc(zT_copied, 1)

            act.wait_ge(const_loaded, CONSTS * 16)
            act.activation(tanh_g[:], gates[:], ACT.Tanh).then_inc(setup_act, 1)
            act.wait_ge(setup_vec, 10)
            act.activation(aw_th[:], aw_lin[:], ACT.Tanh, scale=0.5).then_inc(setup_act, 1)
            copy_max_T(0, 0)

            def body(b, first, last):
                for g in range(NG):
                    late, half = b * 2 - 2 + g // 2, b * 2 - 1 + g // 2
                    for s in range(NT):
                        exp_step(b, g, s)
                        if s == 0:
                            if g % 2 == 0 and not first:
                                exp_scores(late)
                            if g or not first:
                                copy_pv(*before(b, g))
                        if s == 1:
                            if g % 2 == 0 and not first:
                                copy_zT(late)
                            if g < NG - 1:
                                copy_max_T(b, g + 1)
                            elif not last:
                                copy_max_T(b + 1, 0)
                        if s == 2 and (g == 3 or (g == 1 and not first)):
                            copy_hT(half)

            batches(act, body, peeled=2)
            exp_scores(B * 2 - 2)
            copy_pv(B - 1, NG - 1)
            copy_zT(B * 2 - 2)
            copy_hT(B * 2 - 1)
            exp_scores(B * 2 - 1)
            copy_zT(B * 2 - 1)

        @block.vector
        def _(dve):
            def x_stats(b):
                dve.wait_ge(x_loaded, b * 16 + 16)
                wait(dve, xn_done, b * 2)
                for ct in range(NC):
                    dve.bn_stats(stats[:, ct], x_sb[:, ct]).then_inc(stats_done, 1)
                for ct in range(NC):
                    wait_apart(dve, 8 + ct, (stats_done, b * 2 + (ct + 1)))
                    dve.bn_aggr(mv[:, ct], stats[:, ct]).then_inc(mv_done, 1)

            def bias_q(b, ct):
                dve.wait_ge(q_proj, b * 2 + (ct + 1))
                dve.wait_ge(mask_loaded, b * 16 + 16)
                wait(dve, parts_split, (b * 2 + ct) * 4)
                dve.scalar_tensor_tensor(qf[:], bankA[:], bq_sb[:, ct:ct + 1], mask_bc[:], ALU.add, ALU.mult)\
                   .then_inc(q_biased, 1)

            def bias_k(b, ct):
                dve.wait_ge(k_proj, b * 2 + (ct + 1))
                dve.scalar_tensor_tensor(kf[:], bankB[:], bk_sb[:, ct:ct + 1], mask_bc[:], ALU.add, ALU.mult)\
                   .then_inc(k_biased, 1)

            def bias_v(b, i):
                dve.wait_ge(v_proj, b * 2 + (i + 1))
                wait(dve, v_masked_done, b)
                src = (bankA, bankB)[i][:].rearrange("p (s c) -> p s c", s=2)
                dve.tensor_tensor(v_biased[:, 2 * i:2 * i + 2], src,
                                  bv_sb[:].unsqueeze(1).to_broadcast([128, 2, C]), ALU.add)\
                   .then_inc(v_biased_done, 1)

            def max_unit(b, g, u):
                U = (b * NG + g) * UNITS + u
                dve.wait_ge(max_logits, U + 1)
                if u == 0:
                    wait(dve, max_parts, b * NG + g - 1)
                dve.tensor_reduce(neg_max[:, g % 2, u:u + 1], max_bank[u % 2][:], AX_X, ALU.max, negate=True)\
                   .then_inc(max_done, 1)

            def split_max(b, g):
                G = b * NG + g
                dve.wait_ge(max_done, (G + 1) * UNITS)
                wait(dve, max_T, G)
                dve.tensor_copy(neg_max_parts[:, 0:UNITS], neg_max[:, g % 2]).then_inc(max_hi, 1)
                dve.wait_ge(max_hi, G + 1)
                dve.tensor_tensor(neg_max_parts[:, UNITS:], neg_max[:, g % 2],
                                  neg_max_parts[:, 0:UNITS].bitcast(F32), ALU.subtract).then_inc(max_parts, 1)

            def norm_attn(b, g):
                G = b * NG + g
                dve.wait_ge(pv_T, G + 1)
                src = (bankA, bankB)[g % 2 == 0][:].rearrange("p (s j e) -> p s j e", s=NT, j=HG)
                wait(dve, attn_normed, G)
                dve.reciprocal(rsum[:], src[:, :, :, D]).then_inc(norm_step, 1)
                dve.wait_ge(norm_step, G * 2 + 1)
                tm = tm_gate[:, bass.ds(b * NT, NT)].unsqueeze(2).to_broadcast([128, NT, HG])
                dve.tensor_tensor(rscale[:], rsum[:], tm, ALU.mult).then_inc(norm_step, 1)
                dve.wait_ge(norm_step, G * 2 + 2)
                if g % 2 == 0:
                    wait(dve, attn_back, b * 2 + g // 2)
                dst = attn_T[:, :, (g % 2) * 64:(g % 2) * 64 + 64].rearrange("p s (j d) -> p s j d", j=HG)
                dve.tensor_tensor(dst, src[:, :, :, 0:D],
                                  rscale[:].unsqueeze(3).to_broadcast([128, NT, HG, D]), ALU.mult)\
                   .then_inc(attn_normed, 1)

            def add_attn(h):
                dve.wait_ge(attn_back, h + 1)
                dve.wait_ge(xres_loaded, h * 16 + 16)
                wait(dve, h_done, h)
                wait(dve, y_done, h)
                dve.tensor_tensor(xp[:], bankB[:], x_res[:], ALU.add).then_inc(xp_done, 1)
                dve.wait_ge(xp_done, h + 1)
                dve.bn_stats(stats2[:], xp[:]).then_inc(stats2_done, 1)
                wait_apart(dve, 10, (stats2_done, h + 1))
                dve.bn_aggr(mv2[:], stats2[:]).then_inc(mv2_done, 1)

            ROUTER_STEPS = 11

            def router_link(h, n, ins, apart=False):
                ins.then_inc(router_step, 1)
                if apart:
                    wait_apart(dve, 10 + n, (router_step, h * ROUTER_STEPS + n))
                else:
                    dve.wait_ge(router_step, h * ROUTER_STEPS + n)

            def pick(h):
                dve.wait_ge(ffn_in, h + 1)
                router_link(h, 1, dve.tensor_copy(scores[:, 0:E_], bankA[:, 0:E_]), apart=True)
                router_link(h, 2, dve.max(top8[:], scores[:, 0:E_]))
                wait(dve, escore_done, h)
                dve.tensor_scalar(neg_top[:], top8[:, 0:1], -1.0, None, ALU.mult).then_inc(neg_top_done, 1)
                router_link(h, 3, dve.tensor_copy(top2[:, 0:2], top8[:, 0:2]), apart=True)
                router_link(h, 4, dve.match_replace(out=picked[:], in_to_replace=top2[:], in_values=scores[:],
                                                    imm_value=PICK))

            def weigh(h):
                dve.wait_ge(escore_done, h + 1)
                router_link(h, 5, dve.scalar_tensor_tensor(epick[:], picked[:, 0:E_], PICK, escore[:],
                                                           ALU.is_equal, ALU.mult, accum_out=epick_sum[:]))
                router_link(h, 6, dve.scalar_tensor_tensor(eaw[:], epick[:], 1.0, aw[:], ALU.mult, ALU.mult,
                                                           accum_out=eaw_sum[:]))
                router_link(h, 7, dve.scalar_tensor_tensor(den[:], esum[:], 1e-8, epick_sum[:], ALU.mult, ALU.add))
                router_link(h, 8, dve.reciprocal(rden[:], den[:]))
                router_link(h, 9, dve.tensor_scalar(gate_part[:], eaw_sum[:], rden[:], 0.2, ALU.mult, ALU.mult))
                router_link(h, 10, dve.tensor_scalar(wscale[:], gate_part[:], 0.9, rden[:], ALU.add, ALU.mult))
                router_link(h, 11, dve.tensor_scalar(gs[:], epick[:], wscale[:], tanh_g[:, 1:2], ALU.mult, ALU.mult))
                wait(dve, z_T, h)
                dve.tensor_tensor(z[:, 0:S0 * R].rearrange("p (s r) -> p s r", r=R),
                                  bankA[:, E_:FHALF].rearrange("p (s r) -> p s r", r=R),
                                  gs[:, 0:S0].unsqueeze(2).to_broadcast([128, S0, R]), ALU.mult).then_inc(z_done, 1)
                dve.tensor_tensor(z[:, S0 * R:].rearrange("p (s r) -> p s r", r=R),
                                  bankB[:, 0:FHALF].rearrange("p (s r) -> p s r", r=R),
                                  gs[:, S0:].unsqueeze(2).to_broadcast([128, E_ - S0, R]), ALU.mult)\
                   .then_inc(z_done, 1)

            def add_ffn(h):
                dve.wait_ge(ffn_out, h + 1)
                wait(dve, y_stored, h * 16)
                dve.tensor_tensor(y[:], bankB[:], xp[:], ALU.add).then_inc(y_done, 1)

            x_stats(0)
            dve.memset(ka[64:96].bitcast(F32), 0.0).then_inc(zeroed, 1)
            dve.memset(qa[64:96].bitcast(F32), 0.0).then_inc(zeroed, 1)
            dve.memset(ka[96:98].bitcast(F32), 1.0).then_inc(zeroed, 1)
            dve.memset(scores[:], SENT).then_inc(zeroed, 1)
            dve.memset(top2[:], SENT).then_inc(setup_vec, 1)
            dve.wait_ge(const_loaded, CONSTS * 16)
            dve.tensor_scalar(m8_full[:, 0], m8[:], NEG, None, ALU.mult).then_inc(setup_vec, 1)
            dve.tensor_scalar(m8_full[:, 1], m8[:], -1.0, 1.0, ALU.mult, ALU.add).then_inc(setup_vec, 1)
            dve.wait_ge(setup_vec, 3)
            dve.tensor_copy(m8_hi[:], m8_full[:]).then_inc(setup_vec, 1)
            dve.wait_ge(setup_vec, 4)
            dve.tensor_tensor(m8_lo[:], m8_full[:], m8_hi[:].bitcast(F32), ALU.subtract).then_inc(setup_vec, 1)
            dve.tensor_scalar(wq_sb[:], wq_sb[:], 0.25, None, ALU.mult).then_inc(setup_vec, 1)
            dve.tensor_scalar(bq_sb[:], bq_sb[:], 0.25, None, ALU.mult).then_inc(setup_vec, 1)
            dve.wait_ge(setup_vec, 7)
            attr_bc = probs[:, 0, 0:2, :].rearrange("p a t -> p (a t)").rearrange("p (s a) -> p s a", s=E_)
            prod = probs[:, 1, 0:2, :].rearrange("p a t -> p (a t)").rearrange("p (s a) -> p s a", s=E_)
            dve.tensor_tensor(prod, attr_bc, wa_sb[:].unsqueeze(1).to_broadcast([128, E_, E_]), ALU.mult)\
               .then_inc(setup_vec, 1)
            dve.wait_ge(setup_act, 1)
            dve.tensor_scalar(tm_gate[:], mcols[:], tanh_g[:, 0:1], None, ALU.mult).then_inc(setup_vec, 1)
            dve.wait_ge(setup_vec, 9)
            dve.tensor_reduce(aw_lin[:], prod, AX_X, ALU.add).then_inc(setup_vec, 1)
            dve.wait_ge(setup_act, 2)
            dve.tensor_scalar(aw[:], aw_th[:], 0.5, 0.5, ALU.mult, ALU.add).then_inc(setup_vec, 1)
            dve.wait_ge(setup_vec, 11)
            bias_q(0, 0)
            bias_k(0, 0)
            bias_q(0, 1)
            bias_k(0, 1)
            bias_v(0, 0)
            bias_v(0, 1)
            for g in (0, 1):
                for u in range(UNITS):
                    max_unit(0, g, u)
                split_max(0, g)

            def body(b, first, last):
                for g in range(NG):
                    mb, mg = ahead(b, g)
                    late, half = b * 2 - 2 + g // 2, b * 2 - 1 + g // 2
                    for s in range(NT):
                        if not (last and g >= 2):
                            for i in range(4):
                                max_unit(mb, mg, s * 4 + i)
                            if s == NT - 1:
                                split_max(mb, mg)
                        if g % 2 == 0:
                            if s == 0 and not first:
                                weigh(late)
                            if s == 1 and g == 0 and not last:
                                x_stats(b + 1)
                            if s == 2 and not first:
                                add_ffn(late)
                            if s == 2 and not last:
                                bias_q(b + 1, g // 2)
                            if s == 3 and not last:
                                bias_k(b + 1, g // 2)
                            if s == 3 and (g or not first):
                                norm_attn(*before(b, g))
                        else:
                            if s == 0 and (g == 3 or not first):
                                add_attn(half)
                            if s == 0 and g == 1 and not last:
                                bias_v(b + 1, 0)
                            if s == 1:
                                norm_attn(*before(b, g))
                            if s == 2 and g == 1 and not last:
                                bias_v(b + 1, 1)
                            if s == 3 and (g == 3 or not first):
                                pick(half)

            batches(dve, body, peeled=2)
            weigh(B * 2 - 2)
            add_ffn(B * 2 - 2)
            norm_attn(B - 1, NG - 1)
            add_attn(B * 2 - 1)
            pick(B * 2 - 1)
            weigh(B * 2 - 1)
            add_ffn(B * 2 - 1)

        @block.tensor
        def _(pe):
            released = {"A": (zeroed, 0), "B": (zeroed, 0)}

            def take(name, s, value):
                wait(pe, *released[name])
                released[name] = (s, value)

            def project_q(b, ct):
                pe.wait_ge(xn_done, b * 2 + 2)
                take("A", q_biased, b * 2 + (ct + 1))
                for c in range(NC):
                    mm = pe.matmul(bankA[:], wq_sb[:, c, ct * 128:(ct + 1) * 128], xn[:, c],
                                   start=(c == 0), stop=(c == NC - 1))
                mm.then_inc(q_proj, 1)

            def project_k(b, ct):
                pe.wait_ge(ctx_loaded, b * 16 + 16)
                take("B", k_biased, b * 2 + (ct + 1))
                for c in range(NC):
                    mm = pe.matmul(bankB[:], wk_sb[:, c, ct * 128:(ct + 1) * 128], ctx_sb[:, c],
                                   start=(c == 0), stop=(c == NC - 1))
                mm.then_inc(k_proj, 1)

            def project_v(b, i):
                take("AB"[i], v_biased_done, b * 2 + (i + 1))
                dst = (bankA, bankB)[i]
                for s in range(2):
                    for c in range(NC):
                        mm = pe.matmul(dst[:, s * C:(s + 1) * C],
                                       ctx_sb[:, c, (2 * i + s) * 128:(2 * i + s + 1) * 128], wv_sb[:, c],
                                       start=(c == 0), stop=(c == NC - 1))
                mm.then_inc(v_proj, 1)

            def max_unit(b, g, u):
                if u == 0:
                    pe.wait_ge(slot_loaded[g], b * (16 * LOAD_DMAS) + 16 * LOAD_DMAS)
                wait(pe, max_done, (b * NG + g) * UNITS + u - 1)
                j, tt = divmod(u, NT)
                pe.matmul(max_bank[u % 2][:], qa[0:96, g, j, tt * 128:(tt + 1) * 128], ka[0:96, g, j],
                          start=True, stop=True).then_inc(max_logits, 1)

            def exp_unit(b, g, s, j):
                if s == 0 and j == 0:
                    pe.wait_ge(max_loaded[g], b * 16 + 16)
                U = (b * NG + g) * UNITS + (s * HG + j)
                wait(pe, exp_done, U - 1)
                pe.matmul(exp_bank[j % 2][:], ka[0:98, g, j, s * 128:(s + 1) * 128], qa[0:98, g, j],
                          start=True, stop=True).then_inc(exp_logits, 1)

            def pv_half(b, g, s, half):
                G = b * NG + g
                if half == 0:
                    pe.wait_ge(exp_done, (G * NT + s + 1) * HG)
                    if s == 0:
                        pe.wait_ge(v_ready, G + 1)
                        wait(pe, pv_copied, G - 1)
                cols = slice(half * (T // 2), (half + 1) * (T // 2))
                for j in range(HG):
                    mm = pe.matmul(pv_bank[g % 2][32 * j:32 * j + 32, cols], v_ext[:, g, s, j], probs[:, s % 2, j, cols],
                                   start=(s == 0 and half == 0), stop=(s == NT - 1), skip_group_check=True)
                if half == 1:
                    mm.then_inc(pv_step, 1)

            def transpose_max(b, g):
                G = b * NG + g
                pe.wait_ge(max_parts, G + 1)
                take("AB"[g % 2], max_T_copied, G + 1)
                pe.transpose((bankA, bankB)[g % 2][0:2 * UNITS, 0:128], neg_max_parts[:].bitcast(F32), ident[:]).then_inc(max_T, 1)

            def transpose4(dst, tiles, done):
                for k in range(NT):
                    mm = pe.transpose(dst[:, k * 128:(k + 1) * 128], tiles(k), ident[:])
                mm.then_inc(done, 1)

            def transpose_pv(b, g):
                G = b * NG + g
                pe.wait_ge(pv_copied, G + 1)
                odd = g % 2 == 0
                take("AB"[odd], attn_normed, G + 1)
                transpose4((bankA, bankB)[odd], lambda k: pv_sb[:, k * 128:(k + 1) * 128], pv_T)

            def transpose_attn(h):
                pe.wait_ge(attn_normed, h * 2 + 2)
                take("B", xp_done, h + 1)
                transpose4(bankB, lambda k: attn_T[:, k], attn_back)

            def transpose_h(h):
                pe.wait_ge(h_done, h + 1)
                take("A", hT_copied, h + 1)
                transpose4(bankA, lambda k: h_sb[:, k * 128:(k + 1) * 128], h_T)

            def ffn_first(h):
                pe.wait_ge(hT_copied, h + 1)
                take("A", z_done, h * 2 + 1)
                take("B", z_done, h * 2 + 2)
                for n, dst in enumerate((bankA, bankB)):
                    for k in range(NT):
                        mm = pe.matmul(dst[:, 0:FHALF], hT[:, k], wu_sb[:, k, n * FHALF:(n + 1) * FHALF],
                                       start=(k == 0), stop=(k == NT - 1))
                mm.then_inc(ffn_in, 1)

            def transpose_z(h):
                pe.wait_ge(z_done, h * 2 + 2)
                take("A", zT_copied, h + 1)
                transpose4(bankA, lambda k: z[:, k * 128:(k + 1) * 128], z_T)

            def ffn_second(h):
                pe.wait_ge(zT_copied, h + 1)
                take("B", y_done, h + 1)
                for k in range(NT):
                    mm = pe.matmul(bankB[:], zT[:, k], v2_sb[:, k], start=(k == 0), stop=(k == NT - 1))
                mm.then_inc(ffn_out, 1)

            pe.wait_ge(const_loaded, CONSTS * 16)
            pe.wait_ge(setup_vec, 7)
            pe.wait_ge(zeroed, ZEROED)
            pe.wait_ge(ident_ready, 2)
            project_q(0, 0)
            project_k(0, 0)
            project_q(0, 1)
            project_k(0, 1)
            project_v(0, 0)
            project_v(0, 1)
            for g in (0, 1):
                for u in range(UNITS):
                    max_unit(0, g, u)
                if g == 0:
                    transpose_max(0, 0)

            def body(b, first, last):
                if not first:
                    released["A"] = (z_done, b * 4 - 3)
                    released["B"] = (z_done, b * 4 - 2)
                for g in range(NG):
                    mb, mg = ahead(b, g)
                    late, half = b * 2 - 2 + g // 2, b * 2 - 1 + g // 2
                    for s in range(NT):
                        for i in range(4):
                            if not (last and g >= 2):
                                max_unit(mb, mg, s * 4 + i)
                            exp_unit(b, g, s, i)
                            if i % 2 and (s or g or not first):
                                pb, pg = (b, g) if s else before(b, g)
                                pv_half(pb, pg, (s - 1) % NT, i // 2)
                        if g % 2 == 0:
                            if s == 1 and not first:
                                transpose_z(late)
                            if s == 1:
                                transpose_max(b, g + 1)
                            if s == 2 and not first:
                                ffn_second(late)
                            if s == 2 and not last:
                                project_q(b + 1, g // 2)
                            if s == 3 and not last:
                                project_k(b + 1, g // 2)
                            if s == 3 and (g or not first):
                                transpose_pv(*before(b, g))
                        else:
                            if s == 0 and (g == 3 or not first):
                                transpose_attn(half)
                            if s == 0 and g == 1 and not last:
                                project_v(b + 1, 0)
                            if s == 1 and g == 1:
                                transpose_max(b, 2)
                            if s == 1 and g == 3 and not last:
                                transpose_max(b + 1, 0)
                            if s == 1:
                                transpose_pv(*before(b, g))
                            if s == 2 and (g == 3 or not first):
                                transpose_h(half)
                            if s == 2 and g == 1 and not last:
                                project_v(b + 1, 1)
                            if s == 3 and (g == 3 or not first):
                                ffn_first(half)

            batches(pe, body)
            for half in range(2):
                pv_half(B - 1, NG - 1, NT - 1, half)
            transpose_z(B * 2 - 2)
            ffn_second(B * 2 - 2)
            transpose_pv(B - 1, NG - 1)
            transpose_attn(B * 2 - 1)
            transpose_h(B * 2 - 1)
            ffn_first(B * 2 - 1)
            transpose_z(B * 2 - 1)
            ffn_second(B * 2 - 1)


def kernel(**inputs):
    import numpy as np
    import concourse.bacc as bacc
    from concourse.bass_utils import run_bass_kernel_spmd

    a = {k: np.asarray(v) for k, v in inputs.items()}

    def column_tiles(v):
        return v.reshape(-1, 128).T

    named = {
        "x": a["x"].reshape(B * C, T),
        "ctx": a["ctx_2048"].reshape(B * C, T),
        "mask": a["mask_Bx1x2048_fk1"],
        "mask_cols": column_tiles(a["mask_Bx1x2048_fk1"].reshape(-1)),
        "g_x": a["g_xattn"],
        "g_f": a["g_ffn"],
        "wqT": a["L0_xattn_Wq"].T,
        "wkT": a["L0_xattn_Wk"].T,
        "wvT": a["L0_xattn_Wv"].T,
        "bq": column_tiles(a["L0_xattn_bq"]),
        "bk": column_tiles(a["L0_xattn_bk"]),
        "bv": a["L0_xattn_bv"],
        "wu": np.concatenate([a["L0_ffn_Wr"].T, a["L0_ffn_U"].transpose(1, 0, 2).reshape(T, E_ * R)], axis=1),
        "v2": a["L0_ffn_V"].reshape(E_ * R, T),
        "attr": a["L0_ffn_attr"],
        "wa": a["L0_ffn_Wa"],
    }
    nc = bacc.Bacc("TRN2", target_bir_lowering=False, num_devices=1)
    arrays, aps = {}, []
    for name, v in named.items():
        v = np.ascontiguousarray(v)
        arrays["in_" + name] = v
        aps.append(nc.dram_tensor("in_" + name, v.shape, mybir.dt.from_np(v.dtype), kind="ExternalInput").ap())
    out = nc.dram_tensor("out_0", (B * C, T), F32, kind="ExternalOutput").ap()
    build(nc, *aps, out)
    r = run_bass_kernel_spmd(nc, [arrays], core_ids=[0])
    return r.results[0]["out_0"].reshape(B, C, T)
```

```python
import concourse.bass as bass
from concourse import mybir
from contextlib import ExitStack

F32 = mybir.dt.float32
F32R = mybir.dt.float32r
ALU = mybir.AluOpType
ACT = mybir.ActivationFunctionType
AX_X = mybir.AxisListType.X

B, C, T = 8, 256, 512
D = 16
HG = 4
NG = 4
NT = T // 128
NC = C // 128
UNITS = HG * NT
E_, R = 32, 16
WU_COLS = E_ + E_ * R
FHALF = WU_COLS // 2
S0 = (FHALF - E_) // R
NEG = -1000000.0
EPS = 1e-5
LOAD_DMAS = 6
SENT = -3.0e38
PICK = 3.0e38


def build(nc, x, ctx_, mask, mask_cols, g_x, g_f, wqT, wkT, wvT, bq, bk, bv, wu, v2, attr, wa, out):
    with ExitStack() as st_:
        def sb(name, shape, dt=F32):
            return st_.enter_context(nc.sbuf_tensor(name, shape, dt))

        def sem(name):
            return st_.enter_context(nc.semaphore(name))

        def scratch(name, shape):
            return nc.dram_tensor(name, shape, F32, kind="Internal").ap()

        q_parts = scratch("q_parts", (B * NC * 2 * 128, T))
        k_parts = scratch("k_parts", (B * NC * 3 * 128, T))
        q_mask_rows = scratch("q_mask_rows", (B * 4, T))
        k_mask_rows = scratch("k_mask_rows", (B * 4, T))
        max_rows = scratch("max_rows", (B * NG * 32, 128))

        ident = sb("ident", [128, 128])
        wq_lo, wq_hi = sb("wq_lo", [128, NC, C], F32R), sb("wq_hi", [128, NC, C], F32R)
        wk_lo, wk_hi = sb("wk_lo", [128, NC, C], F32R), sb("wk_hi", [128, NC, C], F32R)
        wv_lo, wv_hi = sb("wv_lo", [128, NC, C], F32R), sb("wv_hi", [128, NC, C], F32R)
        wu_lo, wu_hi = sb("wu_lo", [128, NT, WU_COLS], F32R), sb("wu_hi", [128, NT, WU_COLS], F32R)
        v2_lo, v2_hi = sb("v2_lo", [128, NT, T], F32R), sb("v2_hi", [128, NT, T], F32R)
        bq_sb = sb("bq_sb", [128, NC])
        bk_sb = sb("bk_sb", [128, NC])
        bv_sb = sb("bv_sb", [128, C])
        wa_sb = sb("wa_sb", [128, E_])
        gates = sb("gates", [128, 2])
        tanh_g = sb("tanh_g", [128, 2])
        aw = sb("aw", [128, E_])
        aw_lin = sb("aw_lin", [128, E_])
        aw_th = sb("aw_th", [128, E_])
        mcols = sb("mcols", [128, B * NT])
        sm_cols = sb("sm_cols", [128, NT])
        tm_gate = sb("tm_gate", [128, B * NT])
        minus_half = sb("minus_half", [128, NC])
        carrier = sb("carrier", [1, 8])
        eps_sb = sb("eps_sb", [128, NC])
        minus_one = sb("minus_one", [128, NC])
        ones = sb("ones", [128, NT])

        x_sb = sb("x_sb", [128, NC, T])
        xn_hi, xn_lo = sb("xn_hi", [128, NC, T], F32R), sb("xn_lo", [128, NC, T], F32R)
        ctx_sb = sb("ctx_sb", [128, NC, T])
        ctx_hi, ctx_lo = sb("ctx_hi", [128, NC, T], F32R), sb("ctx_lo", [128, NC, T], F32R)
        mask_bc = sb("mask_bc", [128, T])
        qf, kf = sb("qf", [128, T]), sb("kf", [128, T])
        q_hi, q_lo = sb("q_hi", [128, T], F32R), sb("q_lo", [128, T], F32R)
        k_hi, k_lo = sb("k_hi", [128, T], F32R), sb("k_lo", [128, T], F32R)
        qa = sb("qa", [128, NG, HG, T], F32R)
        ka = sb("ka", [128, NG, HG, T], F32R)
        probs = sb("probs", [128, 2, HG, T])
        v_biased = sb("v_biased", [128, NT, C])
        v_ext = sb("v_ext", [128, NG, NT, HG, 32])
        neg_max = sb("neg_max", [128, 2, UNITS])
        neg_max_parts = sb("neg_max_parts", [128, 2 * UNITS], F32R)
        neg_max_T = sb("neg_max_T", [2 * UNITS, 128], F32R)
        pv_sb = sb("pv_sb", [128, T])
        rsum = sb("rsum", [128, NT, HG])
        rscale = sb("rscale", [128, NT, HG])
        attn_T = sb("attn_T", [128, NT, 128])
        x_res = sb("x_res", [128, T])
        xp = sb("xp", [128, T])
        h_sb = sb("h_sb", [128, T])
        hT_hi, hT_lo = sb("hT_hi", [128, T], F32R), sb("hT_lo", [128, T], F32R)
        z = sb("z", [128, T])
        zT_hi, zT_lo = sb("zT_hi", [128, T], F32R), sb("zT_lo", [128, T], F32R)
        y = sb("y", [128, T])
        stats = sb("stats", [128, NC, 6])
        mv = sb("mv", [128, NC, 2])
        rstd = sb("rstd", [128, NC])
        var_eps = sb("var_eps", [128, NC])
        neg_mean = sb("neg_mean", [128, NC])
        shift = sb("shift", [128, NC])
        stats2 = sb("stats2", [128, 6])
        mv2 = sb("mv2", [128, 2])
        rstd2 = sb("rstd2", [128, 1])
        var_eps2 = sb("var_eps2", [128, 1])
        neg_mean2 = sb("neg_mean2", [128, 1])
        shift2 = sb("shift2", [128, 1])
        scores = sb("scores", [128, E_ + 8])
        top8 = sb("top8", [128, 8])
        top2 = sb("top2", [128, 8])
        neg_top = sb("neg_top", [128, 1])
        picked = sb("picked", [128, E_ + 8])
        escore = sb("escore", [128, E_])
        esum = sb("esum", [128, 1])
        epick = sb("epick", [128, E_])
        epick_sum = sb("epick_sum", [128, 1])
        eaw = sb("eaw", [128, E_])
        eaw_sum = sb("eaw_sum", [128, 1])
        den = sb("den", [128, 1])
        rden = sb("rden", [128, 1])
        gate_part = sb("gate_part", [128, 1])
        wscale = sb("wscale", [128, 1])
        gs = sb("gs", [128, E_])

        probs_row = probs[:].rearrange("p a j t -> p (a j t)")
        wu_sb = probs_row[:, 0:NT * WU_COLS].rearrange("p (k n) -> p k n", k=NT)
        attr_wa = probs_row[:, NT * WU_COLS:NT * WU_COLS + E_ * E_]
        attr_sb = v_biased[:].rearrange("p s c -> p (s c)")
        v2_sb = probs_row[:, 0:NT * T].rearrange("p (k t) -> p k t", k=NT)
        wq_sb, wk_sb, wv_sb = (t[:].rearrange("p (c o) -> p c o", c=NC) for t in (x_res, xp, pv_sb))
        m8, m8q, m8k = h_sb[0:B], z[0:B], y[0:B]
        m8q_hi, m8q_lo, m8k_hi, m8k_lo = hT_hi[0:B], hT_lo[0:B], zT_hi[0:B], zT_lo[0:B]

        def bank(name):
            return st_.enter_context(nc.psum_tensor(name, [128, 512], F32))

        max_bank = [bank(f"max_bank{i}") for i in range(3)]
        exp_bank = [bank(f"exp_bank{i}") for i in range(2)]
        pv_bank = bank("pv_bank")
        bankA, bankB = bank("bankA"), bank("bankB")

        q_consts, k_consts, v_consts, f_consts, small_consts = (
            sem(n) for n in ("q_consts", "k_consts", "v_consts", "f_consts", "small_consts"))
        mask_all_loaded = sem("mask_all_loaded")
        zeroed_v, zeroed_p = sem("zeroed_v"), sem("zeroed_p")
        padded = sem("padded")
        ident_ready = sem("ident_ready")
        tanh_done = sem("tanh_done")
        mask_step, aw_step = sem("mask_step"), sem("aw_step")
        bq_scaled = sem("bq_scaled")
        tm_gate_done = sem("tm_gate_done")
        w_hi_done, w_split = sem("w_hi_done"), sem("w_split")
        mask_rows_stored = sem("mask_rows_stored")
        x_loaded = sem("x_loaded")
        ctx_loaded = sem("ctx_loaded")
        mask_loaded = sem("mask_loaded")
        parts_stored = sem("parts_stored")
        slot_loaded = [sem(f"slot_loaded{g}") for g in range(NG)]
        max_stored = sem("max_stored")
        max_loaded = [sem(f"max_loaded{g}") for g in range(NG)]
        xres_loaded = sem("xres_loaded")
        y_stored = sem("y_stored")
        q_proj, k_proj, v_proj = sem("q_proj"), sem("k_proj"), sem("v_proj")
        max_logits, exp_logits = sem("max_logits"), sem("exp_logits")
        pv_step = sem("pv_step")
        max_T, pv_T, attn_back, h_T, ffn_in, z_T, ffn_out = (
            sem(n) for n in ("max_T", "pv_T", "attn_back", "h_T", "ffn_in", "z_T", "ffn_out"))
        exp_done = sem("exp_done")
        max_T_copied, pv_copied, hT_hi_done, zT_hi_done = (
            sem(n) for n in ("max_T_copied", "pv_copied", "hT_hi_done", "zT_hi_done"))
        xn_done, xn_hi_done, ctx_hi_done, h_done = (
            sem(n) for n in ("xn_done", "xn_hi_done", "ctx_hi_done", "h_done"))
        q_biased, k_biased, q_hi_done, k_hi_done = (
            sem(n) for n in ("q_biased", "k_biased", "q_hi_done", "k_hi_done"))
        escore_done = sem("escore_done")
        max_done = sem("max_done")
        max_hi, max_parts = sem("max_hi"), sem("max_parts")
        stats_done, mv_done = sem("stats_done"), sem("mv_done")
        v_biased_done = sem("v_biased_done")
        hT_split, zT_split = sem("hT_split"), sem("zT_split")
        norm_step, attn_normed = sem("norm_step"), sem("attn_normed")
        xp_done, stats2_done, mv2_done = sem("xp_done"), sem("stats2_done"), sem("mv2_done")
        neg_top_done, router_step, z_done, y_done = (
            sem("neg_top_done"), sem("router_step"), sem("z_done"), sem("y_done"))
        ln_step, ln2_step = sem("ln_step"), sem("ln2_step")
        xn_split, ctx_split = sem("xn_split"), sem("ctx_split")
        q_masked, k_masked, q_split, k_split = (
            sem(n) for n in ("q_masked", "k_masked", "q_split", "k_split"))
        sm_ready, v_ready = sem("sm_ready"), sem("v_ready")

        def wait(eng, s, value):
            if isinstance(value, int) and value <= 0:
                return
            eng.wait_ge(s, value)

        def wait_apart(eng, place, *waits):
            for s, value in waits:
                wait(eng, s, value)
            eng.memset(carrier[0:1, place:place + 1], 0.0)

        def before(b, g):
            return (b, g - 1) if g else (b - 1, NG - 1)

        def ahead(b, g):
            return (b, g + 2) if g < 2 else (b + 1, g - 2)

        MAX_BANKS = [v % 3 for v in range(NG * UNITS - 1)] + [1]

        def max_bank_of(g, u):
            return max_bank[MAX_BANKS[g * UNITS + u]]

        def max_bank_age(g, u):
            v = g * UNITS + u
            return next(n for n in range(1, NG * UNITS) if MAX_BANKS[v - n] == MAX_BANKS[v])

        def batches(eng, body, peeled=1):
            for b in range(peeled):
                body(b, b == 0, False)
            with eng.Fori(peeled, B - 1) as b:
                body(b, False, False)
            body(B - 1, False, True)

        block = st_.enter_context(nc.Block())

        @block.sync
        def _(sp):
            def load_x(b):
                wait(sp, xn_split, b * 2)
                rows = x[bass.ds(b * C, C), :]
                sp.dma_start(x_sb[:], rows.rearrange("(c p) t -> p c t", p=128)).then_inc(x_loaded, 16)

            def load_ctx(b):
                wait(sp, ctx_split, b)
                rows = ctx_[bass.ds(b * C, C), :]
                sp.dma_start(ctx_sb[:], rows.rearrange("(c p) t -> p c t", p=128))\
                  .then_inc(ctx_loaded, 16)

            def load_mask(b):
                wait(sp, q_masked, b * 2)
                wait(sp, k_masked, b * 2)
                row = mask[bass.ds(b, 1)].rearrange("b o t -> (b o t)").partition_broadcast(128)
                sp.dma_start(mask_bc[:], row).then_inc(mask_loaded, 16)

            def load_xres(h):
                wait(sp, xp_done, h)
                sp.dma_start(x_res[:], x[bass.ds(h * 128, 128), :]).then_inc(xres_loaded, 16)

            def store_k(b, ct):
                wait(sp, k_split, b * 2 + (ct + 1))
                rows = k_parts[bass.ds((b * NC + ct) * 384, 384), :].rearrange("(r p) t -> p r t", p=128)
                twice = k_hi[:].bitcast(F32).unsqueeze(1).to_broadcast([128, 2, T])
                sp.dma_start(rows[:, 0::2], twice).then_inc(parts_stored, 16)
                sp.dma_start(rows[:, 1], k_lo[:].bitcast(F32)).then_inc(parts_stored, 16)

            def store_q(b, ct):
                wait(sp, q_split, b * 2 + (ct + 1))
                rows = q_parts[bass.ds((b * NC + ct) * 256, 256), :].rearrange("(r p) t -> p r t", p=128)
                sp.dma_start(rows[:, 0], q_hi[:].bitcast(F32)).then_inc(parts_stored, 16)
                sp.dma_start(rows[:, 1], q_lo[:].bitcast(F32)).then_inc(parts_stored, 16)

            def load_slot(b, g):
                wait(sp, parts_stored, b * 128 + (g // 2 + 1) * 64)
                wait(sp, exp_logits, (b * NG + (g + 1 - NG)) * UNITS)
                for side, src, parts, starts in ((qa, q_parts, 2, (0, 0)), (ka, k_parts, 3, (0, 1))):
                    rows = src[bass.ds((b * NC + g // 2) * (parts * 128), parts * 128), :]\
                        .rearrange("(k h) t -> k h t", h=8)
                    heads = slice(g % 2 * HG, g % 2 * HG + HG)
                    for n, start in enumerate(starts):
                        sp.dma_start(side[n * 32:(n + 1) * 32, g].bitcast(F32),
                                     rows[start * D:start * D + 32, heads]).then_inc(slot_loaded[g], 16)
                for side, src in ((qa, q_mask_rows), (ka, k_mask_rows)):
                    rows = src[bass.ds(b * 4, 4), :].unsqueeze(1).to_broadcast([4, HG, T])
                    sp.dma_start(side[64:68, g].bitcast(F32), rows).then_inc(slot_loaded[g], 16)

            def max_to_rows(b, g):
                G = b * NG + g
                wait(sp, max_T_copied, G + 1)
                rows = max_rows[bass.ds(G * 32, 32), :]
                sp.dma_start(rows, neg_max_T[:].bitcast(F32)).then_inc(max_stored, 16)
                wait(sp, max_stored, (G + 1) * 16)
                sp.dma_start(qa[96:98, g].bitcast(F32),
                             rows.rearrange("(h j tt) t -> h j (tt t)", h=2, j=HG)).then_inc(max_loaded[g], 16)

            def store_y(h):
                wait(sp, y_done, h + 1)
                sp.dma_start(out[bass.ds(h * 128, 128), :], y[:]).then_inc(y_stored, 16)

            load_x(0)
            sp.dma_start(wq_sb, wqT.rearrange("(c p) o -> p c o", p=128)).then_inc(q_consts, 16)
            sp.dma_start(bq_sb[:], bq).then_inc(q_consts, 16)
            load_ctx(0)
            sp.dma_start(wk_sb, wkT.rearrange("(c p) o -> p c o", p=128)).then_inc(k_consts, 16)
            sp.dma_start(bk_sb[:], bk).then_inc(k_consts, 16)
            load_mask(0)
            sp.dma_start(m8, mask.rearrange("b o t -> (b o) t")).then_inc(mask_all_loaded, 16)
            sp.dma_start(wv_sb, wvT.rearrange("(c p) o -> p c o", p=128)).then_inc(v_consts, 16)
            sp.dma_start(bv_sb[:], bv.partition_broadcast(128)).then_inc(v_consts, 16)
            for dst, src in ((mcols[:], mask_cols), (gates[:, 0:1], g_x.partition_broadcast(128)),
                             (gates[:, 1:2], g_f.partition_broadcast(128)),
                             (attr_sb, attr.rearrange("s a -> (s a)").partition_broadcast(128)),
                             (wa_sb[:], wa.rearrange("o a -> (o a)").partition_broadcast(128))):
                sp.dma_start(dst, src).then_inc(small_consts, 16)
            sp.dma_start(wu_sb, wu.rearrange("(k p) n -> p k n", p=128)).then_inc(f_consts, 16)
            wait(sp, mask_step, 6)
            for r in range(4):
                sp.dma_start(q_mask_rows.rearrange("(b r) t -> b r t", r=4)[:, r, :],
                             (m8q_hi, m8q_lo)[r % 2].bitcast(F32)).then_inc(mask_rows_stored, 16)
                sp.dma_start(k_mask_rows.rearrange("(b r) t -> b r t", r=4)[:, r, :],
                             (m8k_hi, m8k_lo, m8k_lo, m8k_hi)[r].bitcast(F32)).then_inc(mask_rows_stored, 16)
            wait(sp, mask_rows_stored, 128)
            wait(sp, zeroed_v, NG)
            wait(sp, zeroed_p, NG)
            store_k(0, 0)
            store_q(0, 0)
            load_slot(0, 0)
            load_slot(0, 1)
            wait(sp, w_split, 4)
            sp.dma_start(v2_sb, v2.rearrange("(k p) n -> p k n", p=128)).then_inc(f_consts, 16)
            store_k(0, 1)
            store_q(0, 1)
            load_slot(0, 2)
            load_slot(0, 3)
            load_x(1)
            load_ctx(1)
            load_mask(1)
            max_to_rows(0, 0)

            def body(b, first, last, inputs_left):
                if not first:
                    load_slot(b, 3)
                    load_xres(b * 2 - 1)
                    store_y(b * 2 - 2)
                max_to_rows(b, 1)
                if not last:
                    store_k(b + 1, 0)
                max_to_rows(b, 2)
                if not last:
                    store_q(b + 1, 0)
                    load_slot(b + 1, 0)
                if inputs_left:
                    load_x(b + 2)
                if not last:
                    load_slot(b + 1, 1)
                load_xres(b * 2)
                if not first:
                    store_y(b * 2 - 1)
                max_to_rows(b, 3)
                if not last:
                    store_k(b + 1, 1)
                    max_to_rows(b + 1, 0)
                    store_q(b + 1, 1)
                    load_slot(b + 1, 2)
                if inputs_left:
                    load_ctx(b + 2)
                    load_mask(b + 2)

            body(0, True, False, True)
            with sp.Fori(1, B - 2) as b:
                body(b, False, False, True)
            body(B - 2, False, False, False)
            body(B - 1, False, True, False)
            store_y(B * 2 - 2)
            load_xres(B * 2 - 1)
            store_y(B * 2 - 1)
            sp.wait_ge(y_stored, B * NC * 16)

        @block.gpsimd
        def _(pool):
            pool.memset(minus_half[:], -0.5).then_inc(ident_ready, 1)
            pool.memset(minus_one[:], -1.0).then_inc(ident_ready, 1)
            pool.memset(eps_sb[:], EPS).then_inc(ident_ready, 1)
            pool.memset(ones[:], 1.0).then_inc(ident_ready, 1)
            pool.memset(ident[:], 0.0).then_inc(ident_ready, 1)
            pool.wait_ge(ident_ready, 5)
            pool.affine_select(out=ident[:], in_=ident[:], compare_op=ALU.not_equal, fill=1.0, base=0,
                               pattern=[[-1, 128]], channel_multiplier=1).then_inc(ident_ready, 1)

            def ln_x(b):
                wait(pool, mv_done, b * 2 + 2)
                wait(pool, xn_done, b * 2)
                pool.tensor_tensor(var_eps[:], mv[:, :, 1], eps_sb[:], ALU.add).then_inc(ln_step, 1)
                pool.tensor_tensor(neg_mean[:], mv[:, :, 0], minus_one[:], ALU.mult).then_inc(ln_step, 1)
                pool.wait_ge(ln_step, b * 4 + 2)
                pool.tensor_tensor(rstd[:], var_eps[:], minus_half[:], ALU.pow).then_inc(ln_step, 1)
                pool.wait_ge(ln_step, b * 4 + 3)
                pool.tensor_tensor(shift[:], neg_mean[:], rstd[:], ALU.mult).then_inc(ln_step, 1)

            def ln_xp(h):
                wait(pool, mv2_done, h + 1)
                wait(pool, h_done, h)
                pool.tensor_tensor(var_eps2[:], mv2[:, 1:2], eps_sb[:, 0:1], ALU.add).then_inc(ln2_step, 1)
                pool.tensor_tensor(neg_mean2[:], mv2[:, 0:1], minus_one[:, 0:1], ALU.mult).then_inc(ln2_step, 1)
                pool.wait_ge(ln2_step, h * 4 + 2)
                pool.tensor_tensor(rstd2[:], var_eps2[:], minus_half[:, 0:1], ALU.pow).then_inc(ln2_step, 1)
                pool.wait_ge(ln2_step, h * 4 + 3)
                pool.tensor_tensor(shift2[:], neg_mean2[:], rstd2[:], ALU.mult).then_inc(ln2_step, 1)

            def low_part(lo, full, hi, done):
                pool.tensor_tensor(lo, full, hi.bitcast(F32), ALU.subtract).then_inc(done, 1)

            def split_xn(b):
                wait(pool, q_proj, b * 2)
                for ct in range(NC):
                    pool.wait_ge(xn_hi_done, b * 2 + (ct + 1))
                    low_part(xn_lo[:, ct], x_sb[:, ct], xn_hi[:, ct], xn_split)

            def split_ctx(b):
                pool.wait_ge(ctx_hi_done, b + 1)
                low_part(ctx_lo[:], ctx_sb[:], ctx_hi[:], ctx_split)

            def mask_q(b, ct):
                pool.wait_ge(q_biased, b * 2 + (ct + 1))
                pool.wait_ge(mask_loaded, b * 16 + 16)
                pool.tensor_tensor(qf[:], qf[:], mask_bc[:], ALU.mult).then_inc(q_masked, 1)

            def mask_k(b, ct):
                pool.wait_ge(k_biased, b * 2 + (ct + 1))
                pool.wait_ge(mask_loaded, b * 16 + 16)
                pool.tensor_tensor(kf[:], kf[:], mask_bc[:], ALU.mult).then_inc(k_masked, 1)

            def split_q(b, ct):
                pool.wait_ge(q_hi_done, b * 2 + (ct + 1))
                low_part(q_lo[:], qf[:], q_hi[:], q_split)

            def split_k(b, ct):
                pool.wait_ge(k_hi_done, b * 2 + (ct + 1))
                low_part(k_lo[:], kf[:], k_hi[:], k_split)

            def split_weights(n, full, hi, lo):
                pool.wait_ge(w_hi_done, n)
                low_part(lo[:], full, hi[:], w_split)

            def mask_columns(b):
                wait(pool, v_ready, b * NG)
                pool.tensor_tensor(carrier[0:1, 7:8], minus_half[0:1, 0:1], minus_half[0:1, 0:1], ALU.mult)
                pool.tensor_tensor(sm_cols[:], mcols[:, bass.ds(b * NT, NT)], ones[:], ALU.mult).then_inc(sm_ready, 1)

            def place_v(b, g):
                pool.wait_ge(v_biased_done, b * 2 + 2)
                if g == 0:
                    pool.wait_ge(sm_ready, b + 1)
                wait(pool, pv_step, (b * NG + (g + 1 - NG)) * NT)
                src = v_biased[:, :, g * HG * D:(g + 1) * HG * D].rearrange("p s (j d) -> p s j d", j=HG)
                sm = sm_cols[:].unsqueeze(2).unsqueeze(3).to_broadcast([128, NT, HG, D])
                pool.tensor_tensor(v_ext[:, g, :, :, 0:D], src, sm, ALU.mult).then_inc(v_ready, 1)

            split_weights(1, wq_sb, wq_hi, wq_lo)
            ln_x(0)
            split_xn(0)
            split_weights(2, wk_sb, wk_hi, wk_lo)
            split_ctx(0)
            mask_q(0, 0)
            split_q(0, 0)
            mask_k(0, 0)
            split_k(0, 0)
            pool.wait_ge(k_split, 1)
            for g in range(NG):
                pool.memset(qa[64:96, g].bitcast(F32), 0.0).then_inc(zeroed_p, 1)
            pool.wait_ge(zeroed_p, NG)
            split_weights(3, wv_sb, wv_hi, wv_lo)
            split_weights(4, wu_sb, wu_hi, wu_lo)
            mask_q(0, 1)
            split_q(0, 1)
            mask_k(0, 1)
            split_k(0, 1)
            pool.memset(v_ext[:, :, :, :, D + 1:32], 0.0).then_inc(padded, 1)
            pool.memset(v_ext[:, :, :, :, D:D + 1], 1.0).then_inc(padded, 1)
            pool.wait_ge(small_consts, 80)
            mask_columns(0)
            for g in range(NG - 1):
                place_v(0, g)
            split_weights(5, v2_sb, v2_hi, v2_lo)

            def body(b, first, last):
                place_v(b, NG - 1)
                if not last:
                    split_ctx(b + 1)
                    mask_k(b + 1, 0)
                    ln_x(b + 1)
                    split_k(b + 1, 0)
                    split_xn(b + 1)
                if not first:
                    ln_xp(b * 2 - 1)
                if not last:
                    mask_q(b + 1, 0)
                    split_q(b + 1, 0)
                    mask_columns(b + 1)
                    place_v(b + 1, 0)
                    place_v(b + 1, 1)
                    mask_k(b + 1, 1)
                    split_k(b + 1, 1)
                ln_xp(b * 2)
                if not last:
                    mask_q(b + 1, 1)
                    split_q(b + 1, 1)
                    place_v(b + 1, 2)

            batches(pool, body)
            ln_xp(B * 2 - 1)

        @block.scalar
        def _(act):
            def exp_unit(b, g, s, j):
                S = (b * NG + g) * NT + s
                if j == 0:
                    wait(act, pv_step, S - 1)
                act.wait_ge(exp_logits, S * HG + (j + 1))
                act.activation(probs[:, s % 2, j], exp_bank[j % 2][:], ACT.Exp).then_inc(exp_done, 1)

            def copy_max_T(b, g):
                G = b * NG + g
                act.wait_ge(max_T, G + 1)
                wait(act, max_stored, G * 16)
                act.activation(neg_max_T[:], bankB[0:2 * UNITS, 0:128], ACT.Copy).then_inc(max_T_copied, 1)

            def copy_pv(b, g):
                G = b * NG + g
                act.wait_ge(pv_step, G * NT + NT)
                wait(act, pv_T, G)
                act.activation(pv_sb[:], pv_bank[:], ACT.Copy).then_inc(pv_copied, 1)

            def normalise_x(b):
                act.wait_ge(ln_step, b * 4 + 4)
                for ct in range(NC):
                    act.activation(x_sb[:, ct], x_sb[:, ct], ACT.Identity,
                                   bias=shift[:, ct:ct + 1], scale=rstd[:, ct:ct + 1]).then_inc(xn_done, 1)
                for ct in range(NC):
                    act.wait_ge(xn_done, b * 2 + (ct + 1))
                    wait(act, q_proj, b * 2)
                    act.activation(xn_hi[:, ct], x_sb[:, ct], ACT.Copy).then_inc(xn_hi_done, 1)

            def high_ctx(b):
                act.wait_ge(ctx_loaded, b * 16 + 16)
                wait(act, k_proj, b * 2)
                wait(act, v_proj, b * 2)
                act.activation(ctx_hi[:], ctx_sb[:], ACT.Copy).then_inc(ctx_hi_done, 1)

            def bias_q(b, ct):
                act.wait_ge(q_proj, b * 2 + (ct + 1))
                wait(act, parts_stored, (b * 2 + ct) * 64)
                act.activation(qf[:], bankA[:], ACT.Identity, bias=bq_sb[:, ct:ct + 1], scale=0.25)\
                   .then_inc(q_biased, 1)

            def bias_k(b, ct):
                act.wait_ge(k_proj, b * 2 + (ct + 1))
                wait(act, parts_stored, (b * 2 + ct) * 64)
                act.activation(kf[:], bankB[:], ACT.Identity, bias=bk_sb[:, ct:ct + 1])\
                   .then_inc(k_biased, 1)

            def high_q(b, ct):
                act.wait_ge(q_masked, b * 2 + (ct + 1))
                act.activation(q_hi[:], qf[:], ACT.Copy).then_inc(q_hi_done, 1)

            def high_k(b, ct):
                act.wait_ge(k_masked, b * 2 + (ct + 1))
                act.activation(k_hi[:], kf[:], ACT.Copy).then_inc(k_hi_done, 1)

            def normalise_xp(h):
                act.wait_ge(ln2_step, h * 4 + 4)
                wait(act, h_T, h)
                act.activation(h_sb[:], xp[:], ACT.Identity, bias=shift2[:], scale=rstd2[:]).then_inc(h_done, 1)

            def high_hT(h):
                act.wait_ge(h_T, h + 1)
                wait(act, ffn_in, h)
                act.activation(hT_hi[:], bankA[:], ACT.Copy).then_inc(hT_hi_done, 1)

            def exp_scores(h):
                act.wait_ge(neg_top_done, h + 1)
                act.activation(escore[:], scores[:, 0:E_], ACT.Exp, bias=neg_top[:], accum_out=esum[:])\
                   .then_inc(escore_done, 1)

            def high_zT(h):
                act.wait_ge(z_T, h + 1)
                wait(act, ffn_out, h)
                act.activation(zT_hi[:], bankA[:], ACT.Copy).then_inc(zT_hi_done, 1)

            def high_weights(loaded, value, full, hi):
                act.wait_ge(loaded, value)
                act.activation(hi[:], full, ACT.Copy).then_inc(w_hi_done, 1)

            high_weights(q_consts, 32, wq_sb, wq_hi)
            normalise_x(0)
            high_weights(k_consts, 32, wk_sb, wk_hi)
            high_ctx(0)
            act.wait_ge(bq_scaled, 1)
            bias_q(0, 0)
            bias_k(0, 0)
            high_q(0, 0)
            high_k(0, 0)
            high_weights(v_consts, 32, wv_sb, wv_hi)
            high_weights(f_consts, 16, wu_sb, wu_hi)
            act.wait_ge(small_consts, 80)
            act.activation(tanh_g[:], gates[:], ACT.Tanh).then_inc(tanh_done, 1)
            act.wait_ge(aw_step, 2)
            act.activation(aw_th[:], aw_lin[:], ACT.Tanh, scale=0.5).then_inc(tanh_done, 1)
            bias_q(0, 1)
            bias_k(0, 1)
            high_q(0, 1)
            high_k(0, 1)
            high_weights(f_consts, 32, v2_sb, v2_hi)
            copy_max_T(0, 0)

            def body(b, first, last):
                for g in range(NG):
                    late, half = b * 2 - 2 + g // 2, b * 2 - 1 + g // 2
                    even, ffn = g % 2 == 0, g >= 2 or not first
                    for s in range(NT):
                        if s == 0 and even and not first:
                            high_zT(late)
                        if s == 0 and not even:
                            if not last:
                                bias_q(b + 1, g // 2)
                            if ffn:
                                normalise_xp(half)
                        if s == 1 and even and not last:
                            bias_k(b + 1, g // 2)
                        if s == 1 and not even:
                            if ffn:
                                high_hT(half)
                            if g == 1 or not last:
                                copy_max_T(*((b, 2) if g == 1 else (b + 1, 0)))
                            if not last:
                                high_q(b + 1, g // 2)
                        if s == 2 and even:
                            copy_max_T(b, g + 1)
                            if not last:
                                high_k(b + 1, g // 2)
                                if g == 0:
                                    normalise_x(b + 1)
                        for j in range(HG):
                            exp_unit(b, g, s, j)
                            if s == 2 and j == 2 and not even and ffn:
                                exp_scores(half)
                        if s == 0 and (g or not first):
                            copy_pv(*before(b, g))
                        if s == 0 and g == 0 and not last:
                            high_ctx(b + 1)

            batches(act, body, peeled=2)
            high_zT(B * 2 - 2)
            copy_pv(B - 1, NG - 1)
            normalise_xp(B * 2 - 1)
            high_hT(B * 2 - 1)
            exp_scores(B * 2 - 1)
            high_zT(B * 2 - 1)

        @block.vector
        def _(dve):
            def x_stats(b, ct):
                if ct == 0:
                    dve.wait_ge(x_loaded, b * 16 + 16)
                    wait(dve, xn_done, b * 2)
                dve.bn_stats(stats[:, ct], x_sb[:, ct]).then_inc(stats_done, 1)

            def x_mean_var(b):
                for ct in range(NC):
                    wait_apart(dve, ct, (stats_done, b * 2 + (ct + 1)))
                    dve.bn_aggr(mv[:, ct], stats[:, ct]).then_inc(mv_done, 1)

            def bias_v(b, i):
                dve.wait_ge(v_proj, b * 2 + (i + 1))
                wait(dve, v_ready, b * NG)
                dve.tensor_tensor(v_biased[:, 2 * i:2 * i + 2], bankB[:].rearrange("p (s c) -> p s c", s=2),
                                  bv_sb[:].unsqueeze(1).to_broadcast([128, 2, C]), ALU.add)\
                   .then_inc(v_biased_done, 1)

            def max_unit(b, g, u):
                U = (b * NG + g) * UNITS + u
                dve.wait_ge(max_logits, U + 1)
                if u == 0:
                    wait(dve, max_parts, b * NG + g - 1)
                dve.tensor_reduce(neg_max[:, g % 2, u:u + 1], max_bank_of(g, u)[:], AX_X, ALU.max, negate=True)\
                   .then_inc(max_done, 1)

            def split_max(b, g):
                G = b * NG + g
                dve.wait_ge(max_done, (G + 1) * UNITS)
                wait(dve, max_T, G)
                dve.tensor_copy(neg_max_parts[:, 0:UNITS], neg_max[:, g % 2]).then_inc(max_hi, 1)
                dve.wait_ge(max_hi, G + 1)
                dve.tensor_tensor(neg_max_parts[:, UNITS:], neg_max[:, g % 2],
                                  neg_max_parts[:, 0:UNITS].bitcast(F32), ALU.subtract).then_inc(max_parts, 1)

            def norm_attn(b, g):
                G = b * NG + g
                dve.wait_ge(pv_T, G + 1)
                src = (bankB, bankA)[g % 2][:].rearrange("p (s j e) -> p s j e", s=NT, j=HG)
                wait(dve, attn_normed, G)
                dve.reciprocal(rsum[:], src[:, :, :, D]).then_inc(norm_step, 1)
                dve.wait_ge(norm_step, G * 2 + 1)
                tm = tm_gate[:, bass.ds(b * NT, NT)].unsqueeze(2).to_broadcast([128, NT, HG])
                dve.tensor_tensor(rscale[:], rsum[:], tm, ALU.mult).then_inc(norm_step, 1)
                dve.wait_ge(norm_step, G * 2 + 2)
                if g % 2 == 0:
                    wait(dve, attn_back, b * 2 + g // 2)
                dst = attn_T[:, :, (g % 2) * 64:(g % 2) * 64 + 64].rearrange("p s (j d) -> p s j d", j=HG)
                dve.tensor_tensor(dst, src[:, :, :, 0:D],
                                  rscale[:].unsqueeze(3).to_broadcast([128, NT, HG, D]), ALU.mult)\
                   .then_inc(attn_normed, 1)

            def add_attn(h):
                dve.wait_ge(attn_back, h + 1)
                dve.wait_ge(xres_loaded, h * 16 + 16)
                wait(dve, h_done, h)
                wait(dve, y_done, h)
                dve.tensor_tensor(xp[:], bankA[:], x_res[:], ALU.add).then_inc(xp_done, 1)

            def xp_stats(h):
                dve.wait_ge(xp_done, h + 1)
                dve.bn_stats(stats2[:], xp[:]).then_inc(stats2_done, 1)

            def xp_mean_var(h):
                wait_apart(dve, 2, (stats2_done, h + 1))
                dve.bn_aggr(mv2[:], stats2[:]).then_inc(mv2_done, 1)

            def split_hT(h):
                dve.wait_ge(hT_hi_done, h + 1)
                dve.tensor_tensor(hT_lo[:], bankA[:], hT_hi[:].bitcast(F32), ALU.subtract).then_inc(hT_split, 1)

            def split_zT(h):
                dve.wait_ge(zT_hi_done, h + 1)
                dve.tensor_tensor(zT_lo[:], bankA[:], zT_hi[:].bitcast(F32), ALU.subtract).then_inc(zT_split, 1)

            ROUTER_STEPS = 10

            def router_wait(h, n):
                dve.wait_ge(router_step, h * ROUTER_STEPS + n)

            def pick(h, part):
                if part == 0:
                    dve.wait_ge(ffn_in, h + 1)
                    dve.tensor_copy(scores[:, 0:E_], bankA[:, 0:E_]).then_inc(router_step, 1)
                if part == 1:
                    wait_apart(dve, 3, (router_step, h * ROUTER_STEPS + 1))
                    dve.max(top8[:], scores[:, 0:E_]).then_inc(router_step, 1)
                    router_wait(h, 2)
                    dve.tensor_scalar(neg_top[:], top8[:, 0:1], -1.0, None, ALU.mult).then_inc(neg_top_done, 1)
                    dve.tensor_copy(top2[:, 0:2], top8[:, 0:2]).then_inc(router_step, 1)
                if part == 2:
                    wait_apart(dve, 4, (router_step, h * ROUTER_STEPS + 3))
                    dve.match_replace(out=picked[:], in_to_replace=top2[:], in_values=scores[:],
                                      imm_value=PICK).then_inc(router_step, 1)

            def weigh(h, part):
                if part == 0:
                    router_wait(h, 4)
                    dve.wait_ge(escore_done, h + 1)
                    dve.scalar_tensor_tensor(epick[:], picked[:, 0:E_], PICK, escore[:], ALU.is_equal, ALU.mult,
                                             accum_out=epick_sum[:]).then_inc(router_step, 1)
                    router_wait(h, 5)
                    dve.scalar_tensor_tensor(eaw[:], epick[:], 1.0, aw[:], ALU.mult, ALU.mult,
                                             accum_out=eaw_sum[:])
                    dve.scalar_tensor_tensor(den[:], esum[:], 1e-8, epick_sum[:], ALU.mult, ALU.add)\
                       .then_inc(router_step, 1)
                if part == 1:
                    router_wait(h, 6)
                    dve.reciprocal(rden[:], den[:]).then_inc(router_step, 1)
                    router_wait(h, 7)
                    dve.tensor_scalar(gate_part[:], eaw_sum[:], rden[:], 0.2, ALU.mult, ALU.mult)\
                       .then_inc(router_step, 1)
                if part == 2:
                    router_wait(h, 8)
                    dve.tensor_scalar(wscale[:], gate_part[:], 0.9, rden[:], ALU.add, ALU.mult)\
                       .then_inc(router_step, 1)
                    router_wait(h, 9)
                    dve.tensor_scalar(gs[:], epick[:], wscale[:], tanh_g[:, 1:2], ALU.mult, ALU.mult)\
                       .then_inc(router_step, 1)
                if part == 3:
                    router_wait(h, 10)
                    wait(dve, z_T, h)
                    dve.tensor_tensor(z[:, 0:S0 * R].rearrange("p (s r) -> p s r", r=R),
                                      bankA[:, E_:FHALF].rearrange("p (s r) -> p s r", r=R),
                                      gs[:, 0:S0].unsqueeze(2).to_broadcast([128, S0, R]), ALU.mult)\
                       .then_inc(z_done, 1)
                    dve.tensor_tensor(z[:, S0 * R:].rearrange("p (s r) -> p s r", r=R),
                                      bankB[:, 0:FHALF].rearrange("p (s r) -> p s r", r=R),
                                      gs[:, S0:].unsqueeze(2).to_broadcast([128, E_ - S0, R]), ALU.mult)\
                       .then_inc(z_done, 1)

            def add_ffn(h):
                dve.wait_ge(ffn_out, h + 1)
                wait(dve, y_stored, h * 16)
                dve.tensor_tensor(y[:], bankA[:], xp[:], ALU.add).then_inc(y_done, 1)

            for g in (0, 1):
                dve.memset(ka[64:98, g].bitcast(F32), 1.0).then_inc(zeroed_v, 1)
            for ct in range(NC):
                x_stats(0, ct)
            x_mean_var(0)
            dve.wait_ge(q_consts, 32)
            dve.tensor_scalar(bq_sb[:], bq_sb[:], 0.25, None, ALU.mult).then_inc(bq_scaled, 1)
            dve.wait_ge(mask_all_loaded, 16)
            dve.tensor_scalar(m8q, m8, NEG, None, ALU.mult).then_inc(mask_step, 1)
            dve.tensor_scalar(m8k, m8, -1.0, 1.0, ALU.mult, ALU.add).then_inc(mask_step, 1)
            dve.wait_ge(mask_step, 2)
            dve.tensor_copy(m8q_hi, m8q).then_inc(mask_step, 1)
            dve.tensor_copy(m8k_hi, m8k).then_inc(mask_step, 1)
            dve.wait_ge(mask_step, 4)
            dve.tensor_tensor(m8q_lo, m8q, m8q_hi.bitcast(F32), ALU.subtract).then_inc(mask_step, 1)
            dve.tensor_tensor(m8k_lo, m8k, m8k_hi.bitcast(F32), ALU.subtract).then_inc(mask_step, 1)
            for g in (2, 3):
                dve.memset(ka[64:98, g].bitcast(F32), 1.0).then_inc(zeroed_v, 1)
            dve.memset(scores[:], SENT)
            dve.memset(top2[:], SENT)
            dve.wait_ge(small_consts, 80)
            by_expert = "p (s a) -> p s a"
            dve.tensor_tensor(attr_wa.rearrange(by_expert, s=E_), attr_sb.rearrange(by_expert, s=E_),
                              wa_sb[:].unsqueeze(1).to_broadcast([128, E_, E_]), ALU.mult).then_inc(aw_step, 1)
            dve.wait_ge(aw_step, 1)
            dve.tensor_reduce(aw_lin[:], attr_wa.rearrange(by_expert, s=E_), AX_X, ALU.add).then_inc(aw_step, 1)
            dve.wait_ge(tanh_done, 2)
            dve.tensor_scalar(aw[:], aw_th[:], 0.5, 0.5, ALU.mult, ALU.add).then_inc(aw_step, 1)
            dve.tensor_scalar(tm_gate[:], mcols[:], tanh_g[:, 0:1], None, ALU.mult).then_inc(tm_gate_done, 1)
            for u in range(UNITS):
                max_unit(0, 0, u)
                if u == 4:
                    bias_v(0, 0)
                if u == 8:
                    bias_v(0, 1)
            split_max(0, 0)
            for u in range(UNITS):
                max_unit(0, 1, u)
            split_max(0, 1)

            def body(b, first, last):
                for g in range(NG):
                    mb, mg = ahead(b, g)
                    late, half = b * 2 - 2 + g // 2, b * 2 - 1 + g // 2
                    even, ffn = g % 2 == 0, g >= 2 or not first
                    for s in range(NT):
                        for i in range(4):
                            if not (last and g >= 2):
                                max_unit(mb, mg, s * 4 + i)
                                if s == NT - 1 and i == 3:
                                    split_max(mb, mg)
                            if even:
                                if s == 0 and i == 0 and not first:
                                    split_zT(late)
                                if s == 0 and i == 2 and ffn:
                                    norm_attn(*before(*before(b, g)))
                                if s == 1 and i == 0 and not first:
                                    add_ffn(late)
                                if s == 0 and g == 0 and i in (1, 3) and not last:
                                    x_stats(b + 1, i // 2)
                                if s == 1 and i == 1 and g == 0 and not last:
                                    x_mean_var(b + 1)
                                if s == 2 and i == 0 and ffn:
                                    norm_attn(*before(b, g))
                                if s == 3 and ffn:
                                    if i == 0:
                                        add_attn(half)
                                    if i == 1:
                                        xp_stats(half)
                                    if i == 2:
                                        xp_mean_var(half)
                                if s == 3 and i == 3 and g == 0 and not last:
                                    bias_v(b + 1, 0)
                            else:
                                if s == 0 and i == 0 and g == 1 and not last:
                                    bias_v(b + 1, 1)
                                if s == 1 and i == 1 and ffn:
                                    split_hT(half)
                                if s == 2 and ffn:
                                    pick(half, i)
                                if s == 2 and i == 3 and ffn:
                                    weigh(half, 0)
                                if s == 3 and i < 3 and ffn:
                                    weigh(half, i + 1)

            batches(dve, body, peeled=2)
            split_zT(B * 2 - 2)
            norm_attn(B - 1, NG - 2)
            add_ffn(B * 2 - 2)
            norm_attn(B - 1, NG - 1)
            h = B * 2 - 1
            add_attn(h)
            xp_stats(h)
            xp_mean_var(h)
            split_hT(h)
            for part in range(4):
                pick(h, part)
            for part in range(4):
                weigh(h, part)
            split_zT(h)
            add_ffn(h)

        @block.tensor
        def _(pe):
            released = {"A": (z_done, 0), "B": (z_done, 0)}

            def take(name, s, value):
                wait(pe, *released[name])
                released[name] = (s, value)

            def product(dst, lhs, rhs, done):
                (lhs_hi, lhs_lo), (rhs_hi, rhs_lo) = lhs, rhs
                steps = [(a, r) for c in range(len(lhs_hi))
                         for a, r in ((lhs_hi[c], rhs_hi[c]), (lhs_hi[c], rhs_lo[c]), (lhs_lo[c], rhs_hi[c]))]
                for n, (a, r) in enumerate(steps):
                    mm = pe.matmul(dst, a, r, start=(n == 0), stop=(n == len(steps) - 1))
                if done is not None:
                    mm.then_inc(done, 1)

            def tiles(parts, count, cols=slice(None)):
                return [[t[:, c, cols] for c in range(count)] for t in parts]

            def column_tiles(parts):
                return [[t[:, k * 128:(k + 1) * 128] for k in range(NT)] for t in parts]

            def project_q(b, ct):
                pe.wait_ge(xn_split, b * 2 + 2)
                take("A", q_biased, b * 2 + (ct + 1))
                product(bankA[:], tiles((wq_hi, wq_lo), NC, slice(ct * 128, (ct + 1) * 128)),
                        tiles((xn_hi, xn_lo), NC), q_proj)

            def project_k(b, ct):
                pe.wait_ge(ctx_split, b + 1)
                take("B", k_biased, b * 2 + (ct + 1))
                product(bankB[:], tiles((wk_hi, wk_lo), NC, slice(ct * 128, (ct + 1) * 128)),
                        tiles((ctx_hi, ctx_lo), NC), k_proj)

            def project_v(b, i):
                take("B", v_biased_done, b * 2 + (i + 1))
                for s in range(2):
                    rows = slice((2 * i + s) * 128, (2 * i + s + 1) * 128)
                    product(bankB[:, s * C:(s + 1) * C], tiles((ctx_hi, ctx_lo), NC, rows),
                            tiles((wv_hi, wv_lo), NC), v_proj if s else None)

            def max_unit(b, g, u):
                if u == 0:
                    pe.wait_ge(slot_loaded[g], b * (16 * LOAD_DMAS) + 16 * LOAD_DMAS)
                wait(pe, max_done, (b * NG + g) * UNITS + (u + 1 - max_bank_age(g, u)))
                j, tt = divmod(u, NT)
                pe.matmul(max_bank_of(g, u)[:], qa[0:96, g, j, tt * 128:(tt + 1) * 128], ka[0:96, g, j],
                          start=True, stop=True).then_inc(max_logits, 1)

            def exp_unit(b, g, s, j):
                if s == 0 and j == 0:
                    pe.wait_ge(max_loaded[g], b * 16 + 16)
                U = (b * NG + g) * UNITS + (s * HG + j)
                wait(pe, exp_done, U - 1)
                pe.matmul(exp_bank[j % 2][:], ka[0:98, g, j, s * 128:(s + 1) * 128], qa[0:98, g, j],
                          start=True, stop=True).then_inc(exp_logits, 1)

            def pv_half(b, g, s, half):
                G = b * NG + g
                if half == 0:
                    pe.wait_ge(exp_done, (G * NT + s + 1) * HG)
                    if s == 0:
                        pe.wait_ge(v_ready, G + 1)
                        wait(pe, pv_copied, G)
                cols = slice(half * (T // 2), (half + 1) * (T // 2))
                for j in range(HG):
                    mm = pe.matmul(pv_bank[32 * j:32 * j + 32, cols], v_ext[:, g, s, j], probs[:, s % 2, j, cols],
                                   start=(s == 0 and half == 0), stop=(s == NT - 1), skip_group_check=True)
                if half == 1:
                    mm.then_inc(pv_step, 1)

            def transpose_max(b, g):
                G = b * NG + g
                pe.wait_ge(max_parts, G + 1)
                take("B", max_T_copied, G + 1)
                pe.transpose(bankB[0:2 * UNITS, 0:128], neg_max_parts[:].bitcast(F32), ident[:]).then_inc(max_T, 1)

            def transpose4(dst, tiles, done):
                for k in range(NT):
                    mm = pe.transpose(dst[:, k * 128:(k + 1) * 128], tiles(k), ident[:])
                mm.then_inc(done, 1)

            def transpose_pv(b, g):
                G = b * NG + g
                pe.wait_ge(pv_copied, G + 1)
                take("BA"[g % 2], attn_normed, G + 1)
                transpose4((bankB, bankA)[g % 2], lambda k: pv_sb[:, k * 128:(k + 1) * 128], pv_T)

            def transpose_attn(h):
                pe.wait_ge(attn_normed, h * 2 + 2)
                take("A", xp_done, h + 1)
                transpose4(bankA, lambda k: attn_T[:, k], attn_back)

            def transpose_h(h):
                pe.wait_ge(h_done, h + 1)
                take("A", hT_split, h + 1)
                transpose4(bankA, lambda k: h_sb[:, k * 128:(k + 1) * 128], h_T)

            def ffn_first(h):
                pe.wait_ge(hT_split, h + 1)
                take("A", z_done, h * 2 + 1)
                take("B", z_done, h * 2 + 2)
                for n, dst in enumerate((bankA, bankB)):
                    product(dst[:, 0:FHALF], column_tiles((hT_hi, hT_lo)),
                            tiles((wu_hi, wu_lo), NT, slice(n * FHALF, (n + 1) * FHALF)), ffn_in if n else None)

            def transpose_z(h):
                pe.wait_ge(z_done, h * 2 + 2)
                take("A", zT_split, h + 1)
                transpose4(bankA, lambda k: z[:, k * 128:(k + 1) * 128], z_T)

            def ffn_second(h):
                pe.wait_ge(zT_split, h + 1)
                take("A", y_done, h + 1)
                product(bankA[:], column_tiles((zT_hi, zT_lo)), tiles((v2_hi, v2_lo), NT), ffn_out)

            pe.wait_ge(w_split, 1)
            project_q(0, 0)
            pe.wait_ge(w_split, 2)
            project_k(0, 0)
            project_q(0, 1)
            project_k(0, 1)
            for u in range(UNITS):
                max_unit(0, 0, u)
                if u == 2:
                    pe.wait_ge(w_split, 3)
                    project_v(0, 0)
                if u == 6:
                    project_v(0, 1)
            pe.wait_ge(ident_ready, 6)
            for u in range(UNITS):
                max_unit(0, 1, u)
                if u == 1:
                    transpose_max(0, 0)
            pe.wait_ge(padded, 2)
            pe.wait_ge(w_split, 5)

            def body(b, first, last):
                if not first:
                    released["A"] = (zT_split, b * 2 - 1)
                    released["B"] = (attn_normed, b * 4 - 1)
                for g in range(NG):
                    mb, mg = ahead(b, g)
                    late, half = b * 2 - 2 + g // 2, b * 2 - 1 + g // 2
                    even, ffn = g % 2 == 0, g >= 2 or not first
                    for s in range(NT):
                        for i in range(4):
                            if not (last and g >= 2):
                                max_unit(mb, mg, s * 4 + i)
                            exp_unit(b, g, s, i)
                            if i % 2 and (s or g or not first):
                                pb, pg = (b, g) if s else before(b, g)
                                pv_half(pb, pg, (s - 1) % NT, i // 2)
                        if even:
                            if s == 0 and not first:
                                ffn_second(late)
                            if s == 0 and not last:
                                project_k(b + 1, g // 2)
                            if s == 1 and ffn:
                                transpose_pv(*before(b, g))
                            if s == 1:
                                transpose_max(b, g + 1)
                            if s == 2 and ffn:
                                transpose_attn(half)
                            if s == 2 and g == 0 and not last:
                                project_v(b + 1, 0)
                            if s == 3 and not last:
                                project_q(b + 1, g // 2)
                            if s == 3 and g == 0 and not last:
                                project_v(b + 1, 1)
                        else:
                            if s == 0 and ffn:
                                transpose_h(half)
                            if s == 0 and (g == 1 or not last):
                                transpose_max(*((b, 2) if g == 1 else (b + 1, 0)))
                            if s == 1 and ffn:
                                ffn_first(half)
                            if s == 3 and ffn:
                                transpose_z(half)
                            if s == 3:
                                transpose_pv(*before(b, g))

            batches(pe, body)
            for half in range(2):
                pv_half(B - 1, NG - 1, NT - 1, half)
            ffn_second(B * 2 - 2)
            transpose_pv(B - 1, NG - 1)
            h = B * 2 - 1
            transpose_attn(h)
            transpose_h(h)
            ffn_first(h)
            transpose_z(h)
            ffn_second(h)


def kernel(**inputs):
    import numpy as np
    import concourse.bacc as bacc
    from concourse.bass_utils import run_bass_kernel_spmd

    a = {k: np.asarray(v) for k, v in inputs.items()}

    def column_tiles(v):
        return v.reshape(-1, 128).T

    def by_channel(v):
        return v.reshape(v.shape[:-1] + (NC, 128 // D, D)).swapaxes(-1, -2).reshape(v.shape)

    named = {
        "x": a["x"].reshape(B * C, T),
        "ctx": a["ctx_2048"].reshape(B * C, T),
        "mask": a["mask_Bx1x2048_fk1"],
        "mask_cols": column_tiles(a["mask_Bx1x2048_fk1"].reshape(-1)),
        "g_x": a["g_xattn"],
        "g_f": a["g_ffn"],
        "wqT": by_channel(a["L0_xattn_Wq"].T),
        "wkT": by_channel(a["L0_xattn_Wk"].T),
        "wvT": a["L0_xattn_Wv"].T,
        "bq": column_tiles(by_channel(a["L0_xattn_bq"])),
        "bk": column_tiles(by_channel(a["L0_xattn_bk"])),
        "bv": a["L0_xattn_bv"],
        "wu": np.concatenate([a["L0_ffn_Wr"].T, a["L0_ffn_U"].transpose(1, 0, 2).reshape(T, E_ * R)], axis=1),
        "v2": a["L0_ffn_V"].reshape(E_ * R, T),
        "attr": a["L0_ffn_attr"],
        "wa": a["L0_ffn_Wa"],
    }
    nc = bacc.Bacc("TRN2", target_bir_lowering=False, num_devices=1)
    arrays, aps = {}, []
    for name, v in named.items():
        v = np.ascontiguousarray(v)
        arrays["in_" + name] = v
        aps.append(nc.dram_tensor("in_" + name, v.shape, mybir.dt.from_np(v.dtype), kind="ExternalInput").ap())
    out = nc.dram_tensor("out_0", (B * C, T), F32, kind="ExternalOutput").ap()
    build(nc, *aps, out)
    r = run_bass_kernel_spmd(nc, [arrays], core_ids=[0])
    return r.results[0]["out_0"].reshape(B, C, T)
```

```python
import concourse.bass as bass
from concourse import mybir
from contextlib import ExitStack

F32 = mybir.dt.float32
F32R = mybir.dt.float32r
ALU = mybir.AluOpType
ACT = mybir.ActivationFunctionType
AX_X = mybir.AxisListType.X

B, C, T = 8, 256, 512
D = 16
HG = 4
NG = 4
NT = T // 128
NC = C // 128
UNITS = HG * NT
E_, R = 32, 16
WU_COLS = E_ + E_ * R
FHALF = WU_COLS // 2
S0 = (FHALF - E_) // R
NEG = -1000000.0
EPS = 1e-5
LOAD_DMAS = 6
SENT = -3.0e38
PICK = 3.0e38


def build(nc, x, ctx_, mask, mask_cols, g_x, g_f, wqT, wkT, wvT, bq, bk, bv, wu, v2, attr, wa, out):
    with ExitStack() as st_:
        def sb(name, shape, dt=F32):
            return st_.enter_context(nc.sbuf_tensor(name, shape, dt))

        def sem(name):
            return st_.enter_context(nc.semaphore(name))

        def scratch(name, shape):
            return nc.dram_tensor(name, shape, F32, kind="Internal").ap()

        q_parts = scratch("q_parts", (B * NC * 2 * 128, T))
        k_parts = scratch("k_parts", (B * NC * 3 * 128, T))
        q_mask_rows = scratch("q_mask_rows", (B * 4, T))
        k_mask_rows = scratch("k_mask_rows", (B * 4, T))
        max_rows = scratch("max_rows", (B * NG * 32, 128))

        ident = sb("ident", [128, 128])
        wq_lo, wq_hi = sb("wq_lo", [128, NC, C], F32R), sb("wq_hi", [128, NC, C], F32R)
        wk_lo, wk_hi = sb("wk_lo", [128, NC, C], F32R), sb("wk_hi", [128, NC, C], F32R)
        wv_lo, wv_hi = sb("wv_lo", [128, NC, C], F32R), sb("wv_hi", [128, NC, C], F32R)
        wu_lo, wu_hi = sb("wu_lo", [128, NT, WU_COLS], F32R), sb("wu_hi", [128, NT, WU_COLS], F32R)
        v2_lo, v2_hi = sb("v2_lo", [128, NT, T], F32R), sb("v2_hi", [128, NT, T], F32R)
        bq_sb = sb("bq_sb", [128, NC])
        bk_sb = sb("bk_sb", [128, NC])
        bv_sb = sb("bv_sb", [128, C])
        wa_sb = sb("wa_sb", [128, E_])
        gates = sb("gates", [128, 2])
        tanh_g = sb("tanh_g", [128, 2])
        aw = sb("aw", [128, E_])
        aw_lin = sb("aw_lin", [128, E_])
        aw_th = sb("aw_th", [128, E_])
        mcols = sb("mcols", [128, B * NT])
        sm_cols = sb("sm_cols", [128, NT])
        tm_gate = sb("tm_gate", [128, B * NT])
        minus_half = sb("minus_half", [128, NC])
        carrier = sb("carrier", [1, 8])
        eps_sb = sb("eps_sb", [128, NC])
        minus_one = sb("minus_one", [128, NC])
        ones = sb("ones", [128, NT])

        x_sb = sb("x_sb", [128, NC, T])
        xn_hi, xn_lo = sb("xn_hi", [128, NC, T], F32R), sb("xn_lo", [128, NC, T], F32R)
        ctx_sb = sb("ctx_sb", [128, NC, T])
        ctx_hi, ctx_lo = sb("ctx_hi", [128, NC, T], F32R), sb("ctx_lo", [128, NC, T], F32R)
        mask_bc = sb("mask_bc", [128, T])
        qf, kf = sb("qf", [128, T]), sb("kf", [128, T])
        q_hi, q_lo = sb("q_hi", [128, T], F32R), sb("q_lo", [128, T], F32R)
        k_hi, k_lo = sb("k_hi", [128, T], F32R), sb("k_lo", [128, T], F32R)
        qa = sb("qa", [128, NG, HG, T], F32R)
        ka = sb("ka", [128, NG, HG, T], F32R)
        probs = sb("probs", [128, 2, HG, T])
        v_biased = sb("v_biased", [128, NT, C])
        v_ext = sb("v_ext", [128, NG, NT, HG, 32])
        neg_max = sb("neg_max", [128, 2, UNITS])
        neg_max_parts = sb("neg_max_parts", [128, 2 * UNITS], F32R)
        neg_max_T = sb("neg_max_T", [2 * UNITS, 128], F32R)
        pv_sb = sb("pv_sb", [128, T])
        rsum = sb("rsum", [128, NT, HG])
        rscale = sb("rscale", [128, NT, HG])
        attn_T = sb("attn_T", [128, NT, 128])
        x_res = sb("x_res", [128, T])
        xp = sb("xp", [128, T])
        h_sb = sb("h_sb", [128, T])
        hT_hi, hT_lo = sb("hT_hi", [128, T], F32R), sb("hT_lo", [128, T], F32R)
        z = sb("z", [128, T])
        zT_hi, zT_lo = sb("zT_hi", [128, T], F32R), sb("zT_lo", [128, T], F32R)
        y = sb("y", [128, T])
        stats = sb("stats", [128, NC, 6])
        mv = sb("mv", [128, NC, 2])
        rstd = sb("rstd", [128, NC])
        var_eps = sb("var_eps", [128, NC])
        neg_mean = sb("neg_mean", [128, NC])
        shift = sb("shift", [128, NC])
        stats2 = sb("stats2", [128, 6])
        mv2 = sb("mv2", [128, 2])
        rstd2 = sb("rstd2", [128, 1])
        var_eps2 = sb("var_eps2", [128, 1])
        neg_mean2 = sb("neg_mean2", [128, 1])
        shift2 = sb("shift2", [128, 1])
        scores = sb("scores", [128, E_ + 8])
        top8 = sb("top8", [128, 8])
        top2 = sb("top2", [128, 8])
        neg_top = sb("neg_top", [128, 1])
        picked = sb("picked", [128, E_ + 8])
        escore = sb("escore", [128, E_])
        esum = sb("esum", [128, 1])
        epick = sb("epick", [128, E_])
        epick_sum = sb("epick_sum", [128, 1])
        eaw = sb("eaw", [128, E_])
        eaw_sum = sb("eaw_sum", [128, 1])
        den = sb("den", [128, 1])
        rden = sb("rden", [128, 1])
        gate_part = sb("gate_part", [128, 1])
        wscale = sb("wscale", [128, 1])
        gs = sb("gs", [128, E_])

        probs_row = probs[:].rearrange("p a j t -> p (a j t)")
        wu_sb = probs_row[:, 0:NT * WU_COLS].rearrange("p (k n) -> p k n", k=NT)
        attr_wa = probs_row[:, NT * WU_COLS:NT * WU_COLS + E_ * E_]
        attr_sb = v_biased[:].rearrange("p s c -> p (s c)")
        v2_sb = [t[:] for t in (x_res, xp, pv_sb, attn_T)]
        v2_sb[3] = attn_T[:].rearrange("p s c -> p (s c)")
        wq_sb, wk_sb, wv_sb = (t[:].rearrange("p (c o) -> p c o", c=NC) for t in (x_res, xp, pv_sb))
        m8, m8q, m8k = h_sb[0:B], z[0:B], y[0:B]
        m8q_hi, m8q_lo, m8k_hi, m8k_lo = hT_hi[0:B], hT_lo[0:B], zT_hi[0:B], zT_lo[0:B]

        def bank(name):
            return st_.enter_context(nc.psum_tensor(name, [128, 512], F32))

        max_bank = [bank(f"max_bank{i}") for i in range(3)]
        exp_bank = [bank(f"exp_bank{i}") for i in range(2)]
        pv_bank = bank("pv_bank")
        bankA, bankB = bank("bankA"), bank("bankB")

        q_consts, k_consts, v_consts, wu_loaded, v2_loaded, small_consts = (
            sem(n) for n in ("q_consts", "k_consts", "v_consts", "wu_loaded", "v2_loaded", "small_consts"))
        mask_all_loaded = sem("mask_all_loaded")
        zeroed_v, zeroed_p = sem("zeroed_v"), sem("zeroed_p")
        padded = sem("padded")
        ident_ready = sem("ident_ready")
        tanh_done = sem("tanh_done")
        mask_step, aw_step = sem("mask_step"), sem("aw_step")
        bq_scaled = sem("bq_scaled")
        tm_gate_done = sem("tm_gate_done")
        wq_hi_done, wk_hi_done, wv_hi_done, wu_hi_done, v2_hi_done = (
            sem(n) for n in ("wq_hi_done", "wk_hi_done", "wv_hi_done", "wu_hi_done", "v2_hi_done"))
        wq_split, wk_split, wv_split, wu_split, v2_split = (
            sem(n) for n in ("wq_split", "wk_split", "wv_split", "wu_split", "v2_split"))
        mask_rows_stored = sem("mask_rows_stored")
        x_loaded = sem("x_loaded")
        ctx_loaded = sem("ctx_loaded")
        mask_loaded = sem("mask_loaded")
        q_stored, k_stored = sem("q_stored"), sem("k_stored")
        slot_loaded = [sem(f"slot_loaded{g}") for g in range(NG)]
        max_stored = sem("max_stored")
        max_loaded = [sem(f"max_loaded{g}") for g in range(NG)]
        xres_loaded = sem("xres_loaded")
        y_stored = sem("y_stored")
        q_proj, k_proj, v_proj = sem("q_proj"), sem("k_proj"), sem("v_proj")
        max_logits, exp_logits = sem("max_logits"), sem("exp_logits")
        pv_step = sem("pv_step")
        max_T, pv_T, attn_back, h_T, ffn_in, z_T, ffn_out = (
            sem(n) for n in ("max_T", "pv_T", "attn_back", "h_T", "ffn_in", "z_T", "ffn_out"))
        exp_done = sem("exp_done")
        max_T_copied, pv_copied, hT_hi_done, zT_hi_done = (
            sem(n) for n in ("max_T_copied", "pv_copied", "hT_hi_done", "zT_hi_done"))
        xn_done, xn_hi_done, ctx_hi_done, h_done = (
            sem(n) for n in ("xn_done", "xn_hi_done", "ctx_hi_done", "h_done"))
        q_biased, k_biased, q_hi_done, k_hi_done = (
            sem(n) for n in ("q_biased", "k_biased", "q_hi_done", "k_hi_done"))
        escore_done = sem("escore_done")
        max_done = sem("max_done")
        max_hi, max_parts = sem("max_hi"), sem("max_parts")
        stats_done, mv_done = sem("stats_done"), sem("mv_done")
        v_biased_done = sem("v_biased_done")
        hT_split, zT_split = sem("hT_split"), sem("zT_split")
        norm_step, attn_normed = sem("norm_step"), sem("attn_normed")
        xp_done, stats2_done, mv2_done = sem("xp_done"), sem("stats2_done"), sem("mv2_done")
        neg_top_done, router_step, z_done, y_done = (
            sem("neg_top_done"), sem("router_step"), sem("z_done"), sem("y_done"))
        ln_step, ln2_step = sem("ln_step"), sem("ln2_step")
        xn_split, ctx_split = sem("xn_split"), sem("ctx_split")
        q_masked, k_masked, q_split, k_split = (
            sem(n) for n in ("q_masked", "k_masked", "q_split", "k_split"))
        sm_ready, v_ready = sem("sm_ready"), sem("v_ready")

        def wait(eng, s, value):
            if isinstance(value, int) and value <= 0:
                return
            eng.wait_ge(s, value)

        def wait_apart(eng, place, *waits):
            for s, value in waits:
                wait(eng, s, value)
            eng.memset(carrier[0:1, place:place + 1], 0.0)

        def low_part(eng, lo, full, hi, done):
            eng.tensor_tensor(lo, full, hi.bitcast(F32), ALU.subtract).then_inc(done, 1)

        def before(b, g):
            return (b, g - 1) if g else (b - 1, NG - 1)

        def ahead(b, g):
            return (b, g + 2) if g < 2 else (b + 1, g - 2)

        MAX_BANKS = [v % 3 for v in range(NG * UNITS - 1)] + [1]

        def max_bank_of(g, u):
            return max_bank[MAX_BANKS[g * UNITS + u]]

        def max_bank_age(g, u):
            v = g * UNITS + u
            return next(n for n in range(1, NG * UNITS) if MAX_BANKS[v - n] == MAX_BANKS[v])

        MAX_SHARE = ((0, 1, 1, 2, 3), (1, 1, 2, 1, 0), (1, 1, 1, 0, 1), (1, 1, 0, 1, 1),
                     (0, 1, 1, 1, 0), (1, 1, 1, 1, 1), (0, 1, 0, 1, 0), (1, 0, 0, 1, 0))
        EARLY = 6
        FIRST_SHARE = ((2, 1, 2, 3, 1), (1, 1, 1, 1, 1), (2, 2, 0, 2, 1), (0, 2, 0, 0, 1),
                       (1, 1, 1, 1, 0), (1, 1, 1, 1, 1), (1, 1, 1, 1, 1), (1, 1, 1, 0, 1))
        assert sum(map(sum, MAX_SHARE)) == 2 * UNITS
        assert sum(map(sum, FIRST_SHARE)) == 3 * UNITS - EARLY

        def max_share(b, g, s, i, first):
            opening = first and g < 2
            places = [n for step in (FIRST_SHARE if opening else MAX_SHARE) for n in step]
            place = (g % 2 * NT + s) * 5 + i
            done = sum(places[:place]) + (EARLY if opening else 0)
            for p in range(done, done + places[place]):
                group = p // UNITS
                yield *((b, 1 + group) if opening else ahead(b, g // 2 * 2 + group)), p % UNITS

        def batches(eng, body, peeled=1):
            for b in range(peeled):
                body(b, b == 0, False, True)
            with eng.Fori(peeled, B - 2) as b:
                body(b, False, False, True)
            body(B - 2, False, False, False)
            body(B - 1, False, True, False)

        block = st_.enter_context(nc.Block())

        @block.sync
        def _(sp):
            def load_x(b):
                wait(sp, xn_split, b * 2)
                rows = x[bass.ds(b * C, C), :]
                sp.dma_start(x_sb[:], rows.rearrange("(c p) t -> p c t", p=128)).then_inc(x_loaded, 16)

            def load_ctx(b):
                wait(sp, ctx_split, b * 2)
                rows = ctx_[bass.ds(b * C, C), :]
                sp.dma_start(ctx_sb[:], rows.rearrange("(c p) t -> p c t", p=128))\
                  .then_inc(ctx_loaded, 16)

            def load_mask(b):
                wait(sp, q_masked, b * 2)
                wait(sp, k_masked, b * 2)
                row = mask[bass.ds(b, 1)].rearrange("b o t -> (b o t)").partition_broadcast(128)
                sp.dma_start(mask_bc[:], row).then_inc(mask_loaded, 16)

            def load_xres(h):
                wait(sp, xp_done, h)
                sp.dma_start(x_res[:], x[bass.ds(h * 128, 128), :]).then_inc(xres_loaded, 16)

            def store_k(b, ct):
                wait(sp, k_split, b * 2 + (ct + 1))
                rows = k_parts[bass.ds((b * NC + ct) * 384, 384), :].rearrange("(r p) t -> p r t", p=128)
                twice = k_hi[:].bitcast(F32).unsqueeze(1).to_broadcast([128, 2, T])
                sp.dma_start(rows[:, 0::2], twice).then_inc(k_stored, 16)
                sp.dma_start(rows[:, 1], k_lo[:].bitcast(F32)).then_inc(k_stored, 16)

            def store_q(b, ct):
                wait(sp, q_split, b * 2 + (ct + 1))
                rows = q_parts[bass.ds((b * NC + ct) * 256, 256), :].rearrange("(r p) t -> p r t", p=128)
                sp.dma_start(rows[:, 0], q_hi[:].bitcast(F32)).then_inc(q_stored, 16)
                sp.dma_start(rows[:, 1], q_lo[:].bitcast(F32)).then_inc(q_stored, 16)

            def load_slot_side(b, g, side, src, parts, starts, mask_rows, stored):
                wait(sp, exp_logits, (b * NG + (g + 1 - NG)) * UNITS)
                if isinstance(b, int) and b == 0:
                    wait(sp, zeroed_v, (1, 2, 4, 4)[g])
                    wait(sp, zeroed_p, g + 1)
                rows = mask_rows[bass.ds(b * 4, 4), :].unsqueeze(1).to_broadcast([4, HG, T])
                sp.dma_start(side[64:68, g].bitcast(F32), rows).then_inc(slot_loaded[g], 16)
                wait(sp, stored, b * 64 + (g // 2 + 1) * 32)
                rows = src[bass.ds((b * NC + g // 2) * (parts * 128), parts * 128), :]\
                    .rearrange("(k h) t -> k h t", h=8)
                heads = slice(g % 2 * HG, g % 2 * HG + HG)
                for n, start in enumerate(starts):
                    sp.dma_start(side[n * 32:(n + 1) * 32, g].bitcast(F32),
                                 rows[start * D:start * D + 32, heads]).then_inc(slot_loaded[g], 16)

            def load_slot_k(b, g):
                load_slot_side(b, g, ka, k_parts, 3, (0, 1), k_mask_rows, k_stored)

            def load_slot_q(b, g):
                load_slot_side(b, g, qa, q_parts, 2, (0, 0), q_mask_rows, q_stored)

            def load_slot(b, g):
                load_slot_k(b, g)
                load_slot_q(b, g)

            def max_to_rows(b, g):
                G = b * NG + g
                wait(sp, max_T_copied, G + 1)
                rows = max_rows[bass.ds(G * 32, 32), :]
                sp.dma_start(rows, neg_max_T[:].bitcast(F32)).then_inc(max_stored, 16)
                wait(sp, max_stored, (G + 1) * 16)
                sp.dma_start(qa[96:98, g].bitcast(F32),
                             rows.rearrange("(h j tt) t -> h j (tt t)", h=2, j=HG)).then_inc(max_loaded[g], 16)

            def store_y(h):
                wait(sp, y_done, h + 1)
                sp.dma_start(out[bass.ds(h * 128, 128), :], y[:]).then_inc(y_stored, 16)

            def load_weights(full, src, done):
                sp.dma_start(full, src.rearrange("(c p) o -> p c o", p=128)).then_inc(done, 16)

            load_x(0)
            load_ctx(0)
            load_weights(wk_sb, wkT, k_consts)
            load_weights(wq_sb, wqT, q_consts)
            sp.dma_start(bk_sb[:], bk).then_inc(k_consts, 16)
            sp.dma_start(bq_sb[:], bq).then_inc(q_consts, 16)
            load_mask(0)
            sp.dma_start(m8, mask.rearrange("b o t -> (b o) t")).then_inc(mask_all_loaded, 16)
            load_weights(wv_sb, wvT, v_consts)
            sp.dma_start(bv_sb[:], bv.partition_broadcast(128)).then_inc(v_consts, 16)
            for dst, src in ((mcols[:], mask_cols), (gates[:, 0:1], g_x.partition_broadcast(128)),
                             (gates[:, 1:2], g_f.partition_broadcast(128)),
                             (attr_sb, attr.rearrange("s a -> (s a)").partition_broadcast(128)),
                             (wa_sb[:], wa.rearrange("o a -> (o a)").partition_broadcast(128))):
                sp.dma_start(dst, src).then_inc(small_consts, 16)
            load_weights(wu_sb, wu, wu_loaded)
            wait(sp, mask_step, 6)
            rows = q_mask_rows.rearrange("(b r) t -> b r t", r=4)
            for r, part in enumerate((m8q_hi, m8q_lo)):
                sp.dma_start(rows[:, r::2], part.bitcast(F32).unsqueeze(1).to_broadcast([B, 2, T]))\
                  .then_inc(mask_rows_stored, 16)
            rows = k_mask_rows.rearrange("(b r) t -> b r t", r=4)
            for dst, part in ((rows[:, 0::3], m8k_hi), (rows[:, 1:3], m8k_lo)):
                sp.dma_start(dst, part.bitcast(F32).unsqueeze(1).to_broadcast([B, 2, T]))\
                  .then_inc(mask_rows_stored, 16)
            store_k(0, 0)
            store_q(0, 0)
            wait(sp, mask_rows_stored, 64)
            load_slot(0, 0)
            load_slot(0, 1)
            wait(sp, wq_split, 1)
            wait(sp, wk_split, 1)
            wait(sp, wv_split, 1)
            for k in range(NT):
                sp.dma_start(v2_sb[k], v2[k * 128:(k + 1) * 128, :]).then_inc(v2_loaded, 16)
            load_x(1)
            load_ctx(1)
            store_k(0, 1)
            store_q(0, 1)
            load_slot(0, 2)
            max_to_rows(0, 0)
            load_slot(0, 3)
            load_mask(1)
            wait(sp, v2_split, NT)

            def body(b, first, last, inputs_left):
                if not first:
                    load_slot(b, 3)
                if inputs_left:
                    load_ctx(b + 2)
                if not first:
                    load_xres(b * 2 - 1)
                    store_y(b * 2 - 2)
                max_to_rows(b, 1)
                if not last:
                    store_k(b + 1, 0)
                    store_q(b + 1, 0)
                    load_slot(b + 1, 0)
                max_to_rows(b, 2)
                if inputs_left:
                    load_x(b + 2)
                if not last:
                    load_slot(b + 1, 1)
                load_xres(b * 2)
                if not first:
                    store_y(b * 2 - 1)
                max_to_rows(b, 3)
                if not last:
                    store_k(b + 1, 1)
                    store_q(b + 1, 1)
                    load_slot(b + 1, 2)
                    max_to_rows(b + 1, 0)
                if inputs_left:
                    load_mask(b + 2)

            batches(sp, body)
            load_xres(B * 2 - 1)
            store_y(B * 2 - 2)
            store_y(B * 2 - 1)
            sp.wait_ge(y_stored, B * NC * 16)

        @block.gpsimd
        def _(pool):
            for g in (0, 1):
                pool.memset(qa[64:96, g].bitcast(F32), 0.0).then_inc(zeroed_p, 1)
            pool.wait_ge(zeroed_p, 2)
            pool.memset(minus_half[:], -0.5).then_inc(ident_ready, 1)
            pool.memset(minus_one[:], -1.0).then_inc(ident_ready, 1)
            pool.memset(eps_sb[:], EPS).then_inc(ident_ready, 1)
            pool.memset(ones[:], 1.0).then_inc(ident_ready, 1)
            pool.memset(ident[:], 0.0).then_inc(ident_ready, 1)
            pool.wait_ge(ident_ready, 5)
            pool.affine_select(out=ident[:], in_=ident[:], compare_op=ALU.not_equal, fill=1.0, base=0,
                               pattern=[[-1, 128]], channel_multiplier=1).then_inc(ident_ready, 1)

            def ln_x(b):
                wait(pool, mv_done, b * 2 + 2)
                wait(pool, xn_done, b * 2)
                pool.tensor_tensor(var_eps[:], mv[:, :, 1], eps_sb[:], ALU.add).then_inc(ln_step, 1)
                pool.tensor_tensor(neg_mean[:], mv[:, :, 0], minus_one[:], ALU.mult).then_inc(ln_step, 1)
                pool.wait_ge(ln_step, b * 4 + 2)
                pool.tensor_tensor(rstd[:], var_eps[:], minus_half[:], ALU.pow).then_inc(ln_step, 1)
                pool.wait_ge(ln_step, b * 4 + 3)
                pool.tensor_tensor(shift[:], neg_mean[:], rstd[:], ALU.mult).then_inc(ln_step, 1)

            def ln_xp(h):
                wait(pool, mv2_done, h + 1)
                wait(pool, h_done, h)
                pool.tensor_tensor(var_eps2[:], mv2[:, 1:2], eps_sb[:, 0:1], ALU.add).then_inc(ln2_step, 1)
                pool.tensor_tensor(neg_mean2[:], mv2[:, 0:1], minus_one[:, 0:1], ALU.mult).then_inc(ln2_step, 1)
                pool.wait_ge(ln2_step, h * 4 + 2)
                pool.tensor_tensor(rstd2[:], var_eps2[:], minus_half[:, 0:1], ALU.pow).then_inc(ln2_step, 1)
                pool.wait_ge(ln2_step, h * 4 + 3)
                pool.tensor_tensor(shift2[:], neg_mean2[:], rstd2[:], ALU.mult).then_inc(ln2_step, 1)

            def split_xn(b):
                wait(pool, q_proj, b * 2)
                for ct in range(NC):
                    pool.wait_ge(xn_hi_done, b * 2 + (ct + 1))
                    low_part(pool, xn_lo[:, ct], x_sb[:, ct], xn_hi[:, ct], xn_split)

            def split_ctx(b):
                for c in range(NC):
                    pool.wait_ge(ctx_hi_done, b * 2 + (c + 1))
                    low_part(pool, ctx_lo[:, c], ctx_sb[:, c], ctx_hi[:, c], ctx_split)

            def mask_q(b, ct):
                pool.wait_ge(q_biased, b * 2 + (ct + 1))
                pool.wait_ge(mask_loaded, b * 16 + 16)
                pool.tensor_tensor(qf[:], qf[:], mask_bc[:], ALU.mult).then_inc(q_masked, 1)

            def mask_k(b, ct):
                pool.wait_ge(k_biased, b * 2 + (ct + 1))
                pool.wait_ge(mask_loaded, b * 16 + 16)
                pool.tensor_tensor(kf[:], kf[:], mask_bc[:], ALU.mult).then_inc(k_masked, 1)

            def split_q(b, ct):
                pool.wait_ge(q_hi_done, b * 2 + (ct + 1))
                low_part(pool, q_lo[:], qf[:], q_hi[:], q_split)

            def split_k(b, ct):
                pool.wait_ge(k_hi_done, b * 2 + (ct + 1))
                low_part(pool, k_lo[:], kf[:], k_hi[:], k_split)

            def mask_columns(b):
                wait(pool, v_ready, b * NG)
                pool.tensor_tensor(carrier[0:1, 7:8], minus_half[0:1, 0:1], minus_half[0:1, 0:1], ALU.mult)
                pool.tensor_tensor(sm_cols[:], mcols[:, bass.ds(b * NT, NT)], ones[:], ALU.mult).then_inc(sm_ready, 1)

            def place_v(b, g):
                pool.wait_ge(v_biased_done, b * 2 + 2)
                if g == 0:
                    pool.wait_ge(sm_ready, b + 1)
                wait(pool, pv_step, (b * NG + (g + 1 - NG)) * NT)
                src = v_biased[:, :, g * HG * D:(g + 1) * HG * D].rearrange("p s (j d) -> p s j d", j=HG)
                sm = sm_cols[:].unsqueeze(2).unsqueeze(3).to_broadcast([128, NT, HG, D])
                pool.tensor_tensor(v_ext[:, g, :, :, 0:D], src, sm, ALU.mult).then_inc(v_ready, 1)

            ln_x(0)
            pool.wait_ge(wq_hi_done, 1)
            low_part(pool, wq_lo[:], wq_sb, wq_hi[:], wq_split)
            split_xn(0)
            mask_k(0, 0)
            split_k(0, 0)
            pool.wait_ge(wv_hi_done, 1)
            low_part(pool, wv_lo[:], wv_sb, wv_hi[:], wv_split)
            pool.wait_ge(wv_split, 1)
            for g in (2, 3):
                pool.memset(qa[64:96, g].bitcast(F32), 0.0).then_inc(zeroed_p, 1)
            pool.wait_ge(zeroed_p, NG)
            mask_k(0, 1)
            split_k(0, 1)
            mask_q(0, 1)
            split_q(0, 1)
            pool.memset(v_ext[:, :, :, :, D + 1:32], 0.0).then_inc(padded, 1)
            pool.memset(v_ext[:, :, :, :, D:D + 1], 1.0).then_inc(padded, 1)
            pool.wait_ge(small_consts, 80)
            mask_columns(0)
            for k in range(NT):
                pool.wait_ge(v2_hi_done, k + 1)
                low_part(pool, v2_lo[:, k], v2_sb[k], v2_hi[:, k], v2_split)
            for g in range(NG - 1):
                place_v(0, g)
            ln_x(1)
            split_ctx(1)

            def body(b, first, last, inputs_left):
                place_v(b, NG - 1)
                if not last:
                    mask_k(b + 1, 0)
                    split_xn(b + 1)
                    split_k(b + 1, 0)
                    mask_q(b + 1, 0)
                if not first:
                    ln_xp(b * 2 - 1)
                if not last:
                    split_q(b + 1, 0)
                    mask_columns(b + 1)
                    place_v(b + 1, 0)
                    place_v(b + 1, 1)
                    mask_k(b + 1, 1)
                    split_k(b + 1, 1)
                    mask_q(b + 1, 1)
                ln_xp(b * 2)
                if not last:
                    split_q(b + 1, 1)
                if inputs_left:
                    ln_x(b + 2)
                    split_ctx(b + 2)
                if not last:
                    place_v(b + 1, 2)

            batches(pool, body)
            ln_xp(B * 2 - 1)

        @block.scalar
        def _(act):
            def exp_unit(b, g, s, j):
                S = (b * NG + g) * NT + s
                if j == 0:
                    wait(act, pv_step, S - 1)
                act.wait_ge(exp_logits, S * HG + (j + 1))
                act.activation(probs[:, s % 2, j], exp_bank[j % 2][:], ACT.Exp).then_inc(exp_done, 1)

            def copy_max_T(b, g):
                G = b * NG + g
                act.wait_ge(max_T, G + 1)
                wait(act, max_stored, G * 16)
                act.activation(neg_max_T[:], bankB[0:2 * UNITS, 0:128], ACT.Copy).then_inc(max_T_copied, 1)

            def copy_pv(b, g):
                G = b * NG + g
                act.wait_ge(pv_step, G * NT + NT)
                wait(act, pv_T, G)
                act.activation(pv_sb[:], pv_bank[:], ACT.Copy).then_inc(pv_copied, 1)

            def normalise_x(b, ct):
                act.wait_ge(ln_step, b * 4 + 4)
                act.activation(x_sb[:, ct], x_sb[:, ct], ACT.Identity,
                               bias=shift[:, ct:ct + 1], scale=rstd[:, ct:ct + 1]).then_inc(xn_done, 1)

            def high_xn(b, ct):
                act.wait_ge(xn_done, b * 2 + (ct + 1))
                wait(act, q_proj, b * 2)
                act.activation(xn_hi[:, ct], x_sb[:, ct], ACT.Copy).then_inc(xn_hi_done, 1)

            def high_ctx(b, c):
                act.wait_ge(ctx_loaded, b * 16 + 16)
                wait(act, k_proj, b * 2)
                wait(act, v_proj, b * 2)
                act.activation(ctx_hi[:, c], ctx_sb[:, c], ACT.Copy).then_inc(ctx_hi_done, 1)

            def bias_q(b, ct):
                act.wait_ge(q_proj, b * 2 + (ct + 1))
                wait(act, q_stored, (b * 2 + ct) * 32)
                act.activation(qf[:], bankB[:], ACT.Identity, bias=bq_sb[:, ct:ct + 1], scale=0.25)\
                   .then_inc(q_biased, 1)

            def bias_k(b, ct, bank=bankB):
                act.wait_ge(k_proj, b * 2 + (ct + 1))
                wait(act, k_stored, (b * 2 + ct) * 32)
                act.activation(kf[:], bank[:], ACT.Identity, bias=bk_sb[:, ct:ct + 1])\
                   .then_inc(k_biased, 1)

            def high_q(b, ct):
                act.wait_ge(q_masked, b * 2 + (ct + 1))
                act.activation(q_hi[:], qf[:], ACT.Copy).then_inc(q_hi_done, 1)

            def high_k(b, ct):
                act.wait_ge(k_masked, b * 2 + (ct + 1))
                act.activation(k_hi[:], kf[:], ACT.Copy).then_inc(k_hi_done, 1)

            def normalise_xp(h):
                act.wait_ge(ln2_step, h * 4 + 4)
                wait(act, h_T, h)
                act.activation(h_sb[:], xp[:], ACT.Identity, bias=shift2[:], scale=rstd2[:]).then_inc(h_done, 1)

            def high_hT(h):
                act.wait_ge(h_T, h + 1)
                wait(act, ffn_in, h * 2)
                act.activation(hT_hi[:], bankA[:], ACT.Copy).then_inc(hT_hi_done, 1)

            def exp_scores(h):
                act.wait_ge(neg_top_done, h + 1)
                act.activation(escore[:], scores[:, 0:E_], ACT.Exp, bias=neg_top[:], accum_out=esum[:])\
                   .then_inc(escore_done, 1)

            def high_zT(h):
                act.wait_ge(z_T, h + 1)
                wait(act, ffn_out, h)
                act.activation(zT_hi[:], bankA[:], ACT.Copy).then_inc(zT_hi_done, 1)

            def high_weights(loaded, value, full, hi, done):
                act.wait_ge(loaded, value)
                act.activation(hi, full, ACT.Copy).then_inc(done, 1)

            high_ctx(0, 0)
            high_ctx(0, 1)
            high_weights(k_consts, 32, wk_sb, wk_hi[:], wk_hi_done)
            high_weights(q_consts, 32, wq_sb, wq_hi[:], wq_hi_done)
            normalise_x(0, 0)
            normalise_x(0, 1)
            high_xn(0, 0)
            high_xn(0, 1)
            bias_k(0, 0, bankA)
            high_weights(v_consts, 32, wv_sb, wv_hi[:], wv_hi_done)
            high_k(0, 0)
            act.wait_ge(bq_scaled, 1)
            bias_q(0, 0)
            high_q(0, 0)
            act.wait_ge(small_consts, 80)
            act.activation(tanh_g[:], gates[:], ACT.Tanh).then_inc(tanh_done, 1)
            high_weights(wu_loaded, 16, wu_sb, wu_hi[:], wu_hi_done)
            act.wait_ge(zeroed_v, 3)
            act.activation(ka[64:98, 3], ka[64:98, 2].bitcast(F32), ACT.Copy).then_inc(zeroed_v, 1)
            act.wait_ge(aw_step, 2)
            act.activation(aw_th[:], aw_lin[:], ACT.Tanh, scale=0.5).then_inc(tanh_done, 1)
            bias_k(0, 1, bankA)
            bias_q(0, 1)
            high_k(0, 1)
            high_q(0, 1)
            for k in range(NT):
                high_weights(v2_loaded, 16 * NT, v2_sb[k], v2_hi[:, k], v2_hi_done)
            copy_max_T(0, 0)
            high_ctx(1, 0)
            high_ctx(1, 1)

            def body(b, first, last, inputs_left):
                for g in range(NG):
                    late, half = b * 2 - 2 + g // 2, b * 2 - 1 + g // 2
                    even, ffn = g % 2 == 0, g >= 2 or not first
                    for s in range(NT):
                        for j in range(HG):
                            exp_unit(b, g, s, j)
                            if even:
                                if s == (2 if first and g == 0 else 0) and j == 1:
                                    copy_max_T(b, g + 1)
                                if s == 0 and j == 2 and not first:
                                    high_zT(late)
                                if s == 0 and j == 3 and (g or not first):
                                    copy_pv(*before(b, g))
                                if s == (1 if first else 0) and j < 2 and g == 0 and not last:
                                    normalise_x(b + 1, j)
                                if s == 1 and j in (1, 3) and g == 0 and not last:
                                    high_xn(b + 1, j // 2)
                                if s == 1 and j == 0 and not last:
                                    bias_k(b + 1, g // 2)
                                if s == 2 and j == 1 and not last:
                                    high_k(b + 1, g // 2)
                                if s == 3 and j == 0 and not last:
                                    bias_q(b + 1, g // 2)
                            else:
                                if s == 0 and j == 0 and not last:
                                    high_q(b + 1, g // 2)
                                if s == 0 and j == 1 and ffn:
                                    normalise_xp(half)
                                if s < 2 and j == 2 and g == 3 and inputs_left:
                                    high_ctx(b + 2, s)
                                if s == 0 and j == 3:
                                    copy_pv(*before(b, g))
                                if s == 1 and j == 0 and ffn:
                                    high_hT(half)
                                if s == (2 if first and g == 1 else 1) and j == 1 and (g == 1 or not last):
                                    copy_max_T(*((b, 2) if g == 1 else (b + 1, 0)))
                                if s == 2 and j == 0 and ffn:
                                    exp_scores(half)
                                if s == 3 and j == 2 and g == 3 and last:
                                    high_zT(half)

            batches(act, body, peeled=2)
            copy_pv(B - 1, NG - 1)
            normalise_xp(B * 2 - 1)
            high_hT(B * 2 - 1)
            exp_scores(B * 2 - 1)
            high_zT(B * 2 - 1)

        @block.vector
        def _(dve):
            def x_stats(b, ct):
                if ct == 0:
                    dve.wait_ge(x_loaded, b * 16 + 16)
                    wait(dve, xn_done, b * 2)
                dve.bn_stats(stats[:, ct], x_sb[:, ct]).then_inc(stats_done, 1)

            def x_mean_var(b):
                for ct in range(NC):
                    wait_apart(dve, ct, (stats_done, b * 2 + (ct + 1)))
                    dve.bn_aggr(mv[:, ct], stats[:, ct]).then_inc(mv_done, 1)

            def bias_v(b, i):
                dve.wait_ge(v_proj, b * 2 + (i + 1))
                wait(dve, v_ready, b * NG)
                dve.tensor_tensor(v_biased[:, 2 * i:2 * i + 2], (bankA, bankB)[i][:].rearrange("p (s c) -> p s c", s=2),
                                  bv_sb[:].unsqueeze(1).to_broadcast([128, 2, C]), ALU.add)\
                   .then_inc(v_biased_done, 1)

            def max_unit(b, g, u):
                U = (b * NG + g) * UNITS + u
                dve.wait_ge(max_logits, U + 1)
                if u == 0:
                    wait(dve, max_parts, b * NG + g - 1)
                dve.tensor_reduce(neg_max[:, g % 2, u:u + 1], max_bank_of(g, u)[:], AX_X, ALU.max, negate=True)\
                   .then_inc(max_done, 1)

            def split_max(b, g):
                G = b * NG + g
                dve.wait_ge(max_done, (G + 1) * UNITS)
                wait(dve, max_T, G)
                dve.tensor_copy(neg_max_parts[:, 0:UNITS], neg_max[:, g % 2]).then_inc(max_hi, 1)
                dve.wait_ge(max_hi, G + 1)
                dve.tensor_tensor(neg_max_parts[:, UNITS:], neg_max[:, g % 2],
                                  neg_max_parts[:, 0:UNITS].bitcast(F32), ALU.subtract).then_inc(max_parts, 1)

            def norm_attn(b, g):
                G = b * NG + g
                dve.wait_ge(pv_T, G + 1)
                src = (bankB, bankA)[g % 2][:].rearrange("p (s j e) -> p s j e", s=NT, j=HG)
                wait(dve, attn_normed, G)
                dve.reciprocal(rsum[:], src[:, :, :, D]).then_inc(norm_step, 1)
                dve.wait_ge(norm_step, G * 2 + 1)
                tm = tm_gate[:, bass.ds(b * NT, NT)].unsqueeze(2).to_broadcast([128, NT, HG])
                dve.tensor_tensor(rscale[:], rsum[:], tm, ALU.mult).then_inc(norm_step, 1)
                dve.wait_ge(norm_step, G * 2 + 2)
                if g % 2 == 0:
                    wait(dve, attn_back, b * 2 + g // 2)
                dst = attn_T[:, :, (g % 2) * 64:(g % 2) * 64 + 64].rearrange("p s (j d) -> p s j d", j=HG)
                dve.tensor_tensor(dst, src[:, :, :, 0:D],
                                  rscale[:].unsqueeze(3).to_broadcast([128, NT, HG, D]), ALU.mult)\
                   .then_inc(attn_normed, 1)

            def add_attn(h):
                dve.wait_ge(attn_back, h + 1)
                dve.wait_ge(xres_loaded, h * 16 + 16)
                wait(dve, h_done, h)
                wait(dve, y_done, h)
                dve.tensor_tensor(xp[:], bankA[:], x_res[:], ALU.add).then_inc(xp_done, 1)

            def xp_stats(h):
                dve.wait_ge(xp_done, h + 1)
                dve.bn_stats(stats2[:], xp[:]).then_inc(stats2_done, 1)

            def xp_mean_var(h):
                wait_apart(dve, 2, (stats2_done, h + 1))
                dve.bn_aggr(mv2[:], stats2[:]).then_inc(mv2_done, 1)

            def split_hT(h):
                dve.wait_ge(hT_hi_done, h + 1)
                dve.tensor_tensor(hT_lo[:], bankA[:], hT_hi[:].bitcast(F32), ALU.subtract).then_inc(hT_split, 1)

            def split_zT(h):
                dve.wait_ge(zT_hi_done, h + 1)
                dve.tensor_tensor(zT_lo[:], bankA[:], zT_hi[:].bitcast(F32), ALU.subtract).then_inc(zT_split, 1)

            ROUTER_STEPS = 10

            def router_wait(h, n):
                dve.wait_ge(router_step, h * ROUTER_STEPS + n)

            def pick(h, part):
                if part == 0:
                    dve.wait_ge(ffn_in, h * 2 + 1)
                    dve.tensor_copy(scores[:, 0:E_], bankA[:, 0:E_]).then_inc(router_step, 1)
                if part == 1:
                    wait_apart(dve, 3, (router_step, h * ROUTER_STEPS + 1))
                    dve.max(top8[:], scores[:, 0:E_]).then_inc(router_step, 1)
                    router_wait(h, 2)
                    dve.tensor_scalar(neg_top[:], top8[:, 0:1], -1.0, None, ALU.mult).then_inc(neg_top_done, 1)
                    dve.tensor_copy(top2[:, 0:2], top8[:, 0:2]).then_inc(router_step, 1)
                if part == 2:
                    wait_apart(dve, 4, (router_step, h * ROUTER_STEPS + 3))
                    dve.match_replace(out=picked[:], in_to_replace=top2[:], in_values=scores[:],
                                      imm_value=PICK).then_inc(router_step, 1)

            def weigh(h, part):
                if part == 0:
                    router_wait(h, 4)
                    dve.wait_ge(escore_done, h + 1)
                    dve.scalar_tensor_tensor(epick[:], picked[:, 0:E_], PICK, escore[:], ALU.is_equal, ALU.mult,
                                             accum_out=epick_sum[:]).then_inc(router_step, 1)
                    router_wait(h, 5)
                    dve.scalar_tensor_tensor(eaw[:], epick[:], 1.0, aw[:], ALU.mult, ALU.mult,
                                             accum_out=eaw_sum[:])
                    dve.scalar_tensor_tensor(den[:], esum[:], 1e-8, epick_sum[:], ALU.mult, ALU.add)\
                       .then_inc(router_step, 1)
                if part == 1:
                    router_wait(h, 6)
                    dve.reciprocal(rden[:], den[:]).then_inc(router_step, 1)
                    router_wait(h, 7)
                    dve.tensor_scalar(gate_part[:], eaw_sum[:], rden[:], 0.2, ALU.mult, ALU.mult)\
                       .then_inc(router_step, 1)
                if part == 2:
                    router_wait(h, 8)
                    dve.tensor_scalar(wscale[:], gate_part[:], 0.9, rden[:], ALU.add, ALU.mult)\
                       .then_inc(router_step, 1)
                    router_wait(h, 9)
                    dve.tensor_scalar(gs[:], epick[:], wscale[:], tanh_g[:, 1:2], ALU.mult, ALU.mult)\
                       .then_inc(router_step, 1)
                if part == 3:
                    router_wait(h, 10)
                    wait(dve, z_T, h)
                    dve.wait_ge(ffn_in, h * 2 + 2)
                    dve.tensor_tensor(z[:, 0:S0 * R].rearrange("p (s r) -> p s r", r=R),
                                      bankA[:, E_:FHALF].rearrange("p (s r) -> p s r", r=R),
                                      gs[:, 0:S0].unsqueeze(2).to_broadcast([128, S0, R]), ALU.mult)\
                       .then_inc(z_done, 1)
                    dve.tensor_tensor(z[:, S0 * R:].rearrange("p (s r) -> p s r", r=R),
                                      bankB[:, 0:FHALF].rearrange("p (s r) -> p s r", r=R),
                                      gs[:, S0:].unsqueeze(2).to_broadcast([128, E_ - S0, R]), ALU.mult)\
                       .then_inc(z_done, 1)

            def add_ffn(h):
                dve.wait_ge(ffn_out, h + 1)
                wait(dve, y_stored, h * 16)
                dve.tensor_tensor(y[:], bankA[:], xp[:], ALU.add).then_inc(y_done, 1)

            dve.memset(ka[64:98, 0].bitcast(F32), 1.0).then_inc(zeroed_v, 1)
            for ct in range(NC):
                x_stats(0, ct)
            x_mean_var(0)
            for c in range(NC):
                dve.wait_ge(ctx_hi_done, c + 1)
                low_part(dve, ctx_lo[:, c], ctx_sb[:, c], ctx_hi[:, c], ctx_split)
            dve.wait_ge(wk_hi_done, 1)
            low_part(dve, wk_lo[:], wk_sb, wk_hi[:], wk_split)
            dve.wait_ge(q_consts, 32)
            dve.tensor_scalar(bq_sb[:], bq_sb[:], 0.25, None, ALU.mult).then_inc(bq_scaled, 1)
            dve.wait_ge(mask_all_loaded, 16)
            dve.tensor_scalar(m8q, m8, NEG, None, ALU.mult).then_inc(mask_step, 1)
            dve.tensor_scalar(m8k, m8, -1.0, 1.0, ALU.mult, ALU.add).then_inc(mask_step, 1)
            dve.wait_ge(mask_step, 2)
            dve.tensor_copy(m8q_hi, m8q).then_inc(mask_step, 1)
            dve.tensor_copy(m8k_hi, m8k).then_inc(mask_step, 1)
            dve.wait_ge(mask_step, 4)
            dve.tensor_tensor(m8q_lo, m8q, m8q_hi.bitcast(F32), ALU.subtract).then_inc(mask_step, 1)
            dve.tensor_tensor(m8k_lo, m8k, m8k_hi.bitcast(F32), ALU.subtract).then_inc(mask_step, 1)
            for g in (1, 2):
                dve.memset(ka[64:98, g].bitcast(F32), 1.0).then_inc(zeroed_v, 1)
            dve.wait_ge(q_biased, 1)
            dve.wait_ge(mask_loaded, 16)
            dve.tensor_tensor(qf[:], qf[:], mask_bc[:], ALU.mult).then_inc(q_masked, 1)
            dve.wait_ge(q_hi_done, 1)
            low_part(dve, q_lo[:], qf[:], q_hi[:], q_split)
            dve.memset(scores[:], SENT)
            dve.memset(top2[:], SENT)
            dve.wait_ge(small_consts, 80)
            by_expert = "p (s a) -> p s a"
            dve.tensor_tensor(attr_wa.rearrange(by_expert, s=E_), attr_sb.rearrange(by_expert, s=E_),
                              wa_sb[:].unsqueeze(1).to_broadcast([128, E_, E_]), ALU.mult).then_inc(aw_step, 1)
            dve.wait_ge(aw_step, 1)
            dve.tensor_reduce(aw_lin[:], attr_wa.rearrange(by_expert, s=E_), AX_X, ALU.add).then_inc(aw_step, 1)
            dve.wait_ge(tanh_done, 2)
            dve.tensor_scalar(aw[:], aw_th[:], 0.5, 0.5, ALU.mult, ALU.add).then_inc(aw_step, 1)
            dve.tensor_scalar(tm_gate[:], mcols[:], tanh_g[:, 0:1], None, ALU.mult).then_inc(tm_gate_done, 1)
            for u in range(UNITS):
                max_unit(0, 0, u)
            split_max(0, 0)
            for u in range(EARLY):
                max_unit(0, 1, u)
                if u == 2:
                    bias_v(0, 0)
                if u == 4:
                    bias_v(0, 1)
                if u == 0:
                    dve.wait_ge(wu_hi_done, 1)
                    low_part(dve, wu_lo[:], wu_sb, wu_hi[:], wu_split)
            for ct in range(NC):
                x_stats(1, ct)
            x_mean_var(1)

            def body(b, first, last, inputs_left):
                for g in range(NG):
                    late, half = b * 2 - 2 + g // 2, b * 2 - 1 + g // 2
                    even, ffn = g % 2 == 0, g >= 2 or not first
                    for s in range(NT):
                        for i in range(5):
                            if not (last and g >= 2):
                                for mb, mg, u in max_share(b, g, s, i, first):
                                    max_unit(mb, mg, u)
                                    if u == UNITS - 1:
                                        split_max(mb, mg)
                            if i == 4:
                                continue
                            if even:
                                if s == 0 and i == 0 and ffn:
                                    norm_attn(*before(*before(b, g)))
                                if s == 0 and i == 3 and not first:
                                    split_zT(late)
                                if s == 1 and i == 1 and not first:
                                    add_ffn(late)
                                if s == 2 and i == 0 and ffn:
                                    norm_attn(*before(b, g))
                                if s == 3 and ffn:
                                    if i == 0:
                                        add_attn(half)
                                    if i == 1:
                                        xp_stats(half)
                                    if i == 2:
                                        xp_mean_var(half)
                            else:
                                if s == 0 and i in (0, 2) and g == 1 and not last:
                                    bias_v(b + 1, i // 2)
                                if s == 0 and i in (1, 3) and g == 3 and inputs_left:
                                    x_stats(b + 2, i // 2)
                                if s == 1 and i == 0 and g == 3 and inputs_left:
                                    x_mean_var(b + 2)
                                if s == 1 and i == 1 and ffn:
                                    split_hT(half)
                                if s == 1 and i == 3 and ffn:
                                    pick(half, 0)
                                    pick(half, 1)
                                if s == 2 and i == 0 and ffn:
                                    pick(half, 2)
                                if s == 2 and i == 2 and ffn:
                                    weigh(half, 0)
                                if s == 2 and i == 3 and ffn:
                                    weigh(half, 1)
                                    weigh(half, 2)
                                if s == 3 and i == 0 and ffn:
                                    weigh(half, 3)
                                if s == 3 and i == 3 and g == 3 and last:
                                    split_zT(half)

            batches(dve, body, peeled=2)
            norm_attn(B - 1, NG - 2)
            add_ffn(B * 2 - 2)
            norm_attn(B - 1, NG - 1)
            h = B * 2 - 1
            add_attn(h)
            xp_stats(h)
            xp_mean_var(h)
            split_hT(h)
            for part in range(4):
                pick(h, part)
            for part in range(4):
                weigh(h, part)
            split_zT(h)
            add_ffn(h)

        @block.tensor
        def _(pe):
            released = {"A": (z_done, 0), "B": (z_done, 0)}

            def take(name, s, value):
                wait(pe, *released[name])
                released[name] = (s, value)

            def product(dst, lhs, rhs, done):
                (lhs_hi, lhs_lo), (rhs_hi, rhs_lo) = lhs, rhs
                steps = [(a, r) for c in range(len(lhs_hi))
                         for a, r in ((lhs_hi[c], rhs_hi[c]), (lhs_hi[c], rhs_lo[c]), (lhs_lo[c], rhs_hi[c]))]
                for n, (a, r) in enumerate(steps):
                    mm = pe.matmul(dst, a, r, start=(n == 0), stop=(n == len(steps) - 1))
                if done is not None:
                    mm.then_inc(done, 1)

            def tiles(parts, count, cols=slice(None)):
                return [[t[:, c, cols] for c in range(count)] for t in parts]

            def column_tiles(parts):
                return [[t[:, k * 128:(k + 1) * 128] for k in range(NT)] for t in parts]

            def project_q(b, ct):
                pe.wait_ge(xn_split, b * 2 + 2)
                take("B", q_biased, b * 2 + (ct + 1))
                product(bankB[:], tiles((wq_hi, wq_lo), NC, slice(ct * 128, (ct + 1) * 128)),
                        tiles((xn_hi, xn_lo), NC), q_proj)

            def project_k(b, ct, name="B"):
                pe.wait_ge(ctx_split, b * 2 + 2)
                take(name, k_biased, b * 2 + (ct + 1))
                product((bankA if name == "A" else bankB)[:], tiles((wk_hi, wk_lo), NC, slice(ct * 128, (ct + 1) * 128)),
                        tiles((ctx_hi, ctx_lo), NC), k_proj)

            def project_v(b, i):
                take("AB"[i], v_biased_done, b * 2 + (i + 1))
                for s in range(2):
                    rows = slice((2 * i + s) * 128, (2 * i + s + 1) * 128)
                    product((bankA, bankB)[i][:, s * C:(s + 1) * C], tiles((ctx_hi, ctx_lo), NC, rows),
                            tiles((wv_hi, wv_lo), NC), v_proj if s else None)

            def max_unit(b, g, u):
                if u == 0:
                    pe.wait_ge(slot_loaded[g], b * (16 * LOAD_DMAS) + 16 * LOAD_DMAS)
                wait(pe, max_done, (b * NG + g) * UNITS + (u + 1 - max_bank_age(g, u)))
                j, tt = divmod(u, NT)
                pe.matmul(max_bank_of(g, u)[:], qa[0:96, g, j, tt * 128:(tt + 1) * 128], ka[0:96, g, j],
                          start=True, stop=True).then_inc(max_logits, 1)

            def exp_unit(b, g, s, j):
                if s == 0 and j == 0:
                    pe.wait_ge(max_loaded[g], b * 16 + 16)
                U = (b * NG + g) * UNITS + (s * HG + j)
                wait(pe, exp_done, U - 1)
                pe.matmul(exp_bank[j % 2][:], ka[0:98, g, j, s * 128:(s + 1) * 128], qa[0:98, g, j],
                          start=True, stop=True).then_inc(exp_logits, 1)

            def probs_v(b, g, s):
                G = b * NG + g
                pe.wait_ge(exp_done, (G * NT + s + 1) * HG)
                if s == 0:
                    pe.wait_ge(v_ready, G + 1)
                    wait(pe, pv_copied, G)
                for j in range(HG):
                    mm = pe.matmul(pv_bank[32 * j:32 * j + 32], v_ext[:, g, s, j], probs[:, s % 2, j],
                                   start=(s == 0), stop=(s == NT - 1), skip_group_check=True)
                mm.then_inc(pv_step, 1)

            def transpose_max(b, g):
                G = b * NG + g
                pe.wait_ge(max_parts, G + 1)
                take("B", max_T_copied, G + 1)
                pe.transpose(bankB[0:2 * UNITS, 0:128], neg_max_parts[:].bitcast(F32), ident[:]).then_inc(max_T, 1)

            def transpose4(dst, tiles, done):
                for k in range(NT):
                    mm = pe.transpose(dst[:, k * 128:(k + 1) * 128], tiles(k), ident[:])
                mm.then_inc(done, 1)

            def transpose_pv(b, g):
                G = b * NG + g
                pe.wait_ge(pv_copied, G + 1)
                take("BA"[g % 2], attn_normed, G + 1)
                transpose4((bankB, bankA)[g % 2], lambda k: pv_sb[:, k * 128:(k + 1) * 128], pv_T)

            def transpose_attn(h):
                pe.wait_ge(attn_normed, h * 2 + 2)
                take("A", xp_done, h + 1)
                transpose4(bankA, lambda k: attn_T[:, k], attn_back)

            def transpose_h(h):
                pe.wait_ge(h_done, h + 1)
                take("A", hT_split, h + 1)
                transpose4(bankA, lambda k: h_sb[:, k * 128:(k + 1) * 128], h_T)

            def ffn_first(h, n):
                if n == 0:
                    pe.wait_ge(hT_split, h + 1)
                take("AB"[n], z_done, h * 2 + n + 1)
                product((bankA, bankB)[n][:, 0:FHALF], column_tiles((hT_hi, hT_lo)),
                        tiles((wu_hi, wu_lo), NT, slice(n * FHALF, (n + 1) * FHALF)), ffn_in)

            def transpose_z(h):
                pe.wait_ge(z_done, h * 2 + 2)
                take("A", zT_split, h + 1)
                transpose4(bankA, lambda k: z[:, k * 128:(k + 1) * 128], z_T)

            def ffn_second(h):
                pe.wait_ge(zT_split, h + 1)
                take("A", y_done, h + 1)
                product(bankA[:], column_tiles((zT_hi, zT_lo)), tiles((v2_hi, v2_lo), NT), ffn_out)

            pe.wait_ge(wk_split, 1)
            project_k(0, 0, "A")
            pe.wait_ge(wq_split, 1)
            project_q(0, 0)
            project_k(0, 1, "A")
            project_q(0, 1)
            for u in range(UNITS):
                max_unit(0, 0, u)
            pe.wait_ge(ident_ready, 6)
            for u in range(EARLY):
                max_unit(0, 1, u)
                if u == 0:
                    pe.wait_ge(wv_split, 1)
                    project_v(0, 0)
                if u == 1:
                    transpose_max(0, 0)
                if u == 3:
                    project_v(0, 1)
            pe.wait_ge(padded, 2)
            pe.wait_ge(wu_split, 1)

            def body(b, first, last, inputs_left):
                if not first:
                    released["A"] = (z_done, b * 4 - 3)
                    released["B"] = (attn_normed, b * 4 - 1)
                for g in range(NG):
                    late, half = b * 2 - 2 + g // 2, b * 2 - 1 + g // 2
                    even, ffn = g % 2 == 0, g >= 2 or not first
                    if first and g == 1:
                        pe.wait_ge(v2_split, NT)
                    for s in range(NT):
                        def max_units(i):
                            if not (last and g >= 2):
                                for unit in max_share(b, g, s, i, first):
                                    max_unit(*unit)

                        for i in range(4):
                            max_units(i)
                            if even and s == (2 if first and g == 0 else 0) and i == 2:
                                transpose_max(b, g + 1)
                            exp_unit(b, g, s, i)
                            if i == 1 and (s or g or not first):
                                pb, pg = (b, g) if s else before(b, g)
                                probs_v(pb, pg, (s - 1) % NT)
                            if even and s == 0 and i == 1 and not first:
                                transpose_z(late)
                            if not even and s == 1 and i == 2 and ffn:
                                ffn_first(half, 0)
                            if s == 3 and i == 1 and g == 3 and last:
                                transpose_z(half)
                        if even:
                            if s == 0 and not last:
                                project_k(b + 1, g // 2)
                            if s == 1 and ffn:
                                transpose_pv(*before(b, g))
                            if s == 2 and ffn:
                                transpose_attn(half)
                            if s == 3 and g == 0 and not last:
                                project_v(b + 1, 0)
                        elif ffn and s == 0:
                            transpose_h(half)
                        max_units(4)
                        if even:
                            if s == 0 and not first:
                                ffn_second(late)
                            if s == 2 and not last:
                                project_q(b + 1, g // 2)
                            if s == 3 and g == 0 and not last:
                                project_v(b + 1, 1)
                        else:
                            if s == (1 if first and g == 1 else 0) and (g == 1 or not last):
                                transpose_max(*((b, 2) if g == 1 else (b + 1, 0)))
                            if s == 1 and ffn:
                                ffn_first(half, 1)
                            if s == 3:
                                transpose_pv(*before(b, g))
                            if s == 3 and g == 3 and last:
                                ffn_second(half)

            batches(pe, body)
            probs_v(B - 1, NG - 1, NT - 1)
            transpose_pv(B - 1, NG - 1)
            h = B * 2 - 1
            transpose_attn(h)
            transpose_h(h)
            ffn_first(h, 0)
            ffn_first(h, 1)
            transpose_z(h)
            ffn_second(h)


def kernel(**inputs):
    import numpy as np
    import concourse.bacc as bacc
    from concourse.bass_utils import run_bass_kernel_spmd

    a = {k: np.asarray(v) for k, v in inputs.items()}

    def column_tiles(v):
        return v.reshape(-1, 128).T

    def by_channel(v):
        return v.reshape(v.shape[:-1] + (NC, 128 // D, D)).swapaxes(-1, -2).reshape(v.shape)

    named = {
        "x": a["x"].reshape(B * C, T),
        "ctx": a["ctx_2048"].reshape(B * C, T),
        "mask": a["mask_Bx1x2048_fk1"],
        "mask_cols": column_tiles(a["mask_Bx1x2048_fk1"].reshape(-1)),
        "g_x": a["g_xattn"],
        "g_f": a["g_ffn"],
        "wqT": by_channel(a["L0_xattn_Wq"].T),
        "wkT": by_channel(a["L0_xattn_Wk"].T),
        "wvT": a["L0_xattn_Wv"].T,
        "bq": column_tiles(by_channel(a["L0_xattn_bq"])),
        "bk": column_tiles(by_channel(a["L0_xattn_bk"])),
        "bv": a["L0_xattn_bv"],
        "wu": np.concatenate([a["L0_ffn_Wr"].T, a["L0_ffn_U"].transpose(1, 0, 2).reshape(T, E_ * R)], axis=1),
        "v2": a["L0_ffn_V"].reshape(E_ * R, T),
        "attr": a["L0_ffn_attr"],
        "wa": a["L0_ffn_Wa"],
    }
    nc = bacc.Bacc("TRN2", target_bir_lowering=False, num_devices=1)
    arrays, aps = {}, []
    for name, v in named.items():
        v = np.ascontiguousarray(v)
        arrays["in_" + name] = v
        aps.append(nc.dram_tensor("in_" + name, v.shape, mybir.dt.from_np(v.dtype), kind="ExternalInput").ap())
    out = nc.dram_tensor("out_0", (B * C, T), F32, kind="ExternalOutput").ap()
    build(nc, *aps, out)
    r = run_bass_kernel_spmd(nc, [arrays], core_ids=[0])
    return r.results[0]["out_0"].reshape(B, C, T)
```
